# Optimizing a Trainium2 kernel written in Bass

```python
import numpy as np
import jax
import jax.numpy as jnp

def _softmax(x, axis=-1):
    return jax.nn.softmax(x, axis=axis)

def _gelu(x):
    return jax.nn.gelu(x, approximate=True)

def _silu(x):
    return jax.nn.silu(x)

def _sigmoid(x):
    return jax.nn.sigmoid(x)

def _layernorm(x, axis=-1, eps=1e-05):
    m = jnp.mean(x, axis=axis, keepdims=True)
    v = jnp.var(x, axis=axis, keepdims=True)
    return (x - m) / jnp.sqrt(v + eps)

def _scatter_add(tgt, idx, src, axis=0):
    return tgt.at[idx].add(src)

def _segment_sum(src, seg, n):
    return jax.ops.segment_sum(src, seg, n)
kernel_name = 'mk_seq_postln_d2_jaxref_r8_584bde'

def setup_inputs(seed: int=0):
    np.random.seed(seed)
    _w = jnp.asarray

    def _L0_attn_setup():
        import jax, jax.numpy as jnp
        import numpy as np
        N_EMBD = 128
        N_HEAD = 16
        HEAD_DIM = N_EMBD // N_HEAD
        ROPE_THETA = 10000.0

        def _rope_cos_sin(seq_len, dim, dtype):
            inv_freq = 1.0 / ROPE_THETA ** (jnp.arange(0, dim, 2, dtype=jnp.float32) / dim)
            ang = jnp.arange(seq_len, dtype=jnp.float32)[:, None] * inv_freq[None, :]
            cos = jnp.concatenate([jnp.cos(ang), jnp.cos(ang)], axis=-1).astype(dtype)
            sin = jnp.concatenate([jnp.sin(ang), jnp.sin(ang)], axis=-1).astype(dtype)
            return (cos, sin)

        def _rotate_half(t):
            d = t.shape[-1] // 2
            return jnp.concatenate([-t[..., d:], t[..., :d]], axis=-1)
        key = jax.random.key(seed)
        k1, k2, k3 = jax.random.split(key, 3)
        B, S = (2, 256)
        x = jax.random.normal(k1, (B, S, N_EMBD), dtype=jnp.float32)
        w_qkv = jax.random.normal(k2, (N_EMBD, 3 * N_EMBD), dtype=jnp.float32) * (1.0 / np.sqrt(N_EMBD))
        w_out = jax.random.normal(k3, (N_EMBD, N_EMBD), dtype=jnp.float32) * (1.0 / np.sqrt(N_EMBD))
        return {'x': x, 'w_qkv': w_qkv, 'w_out': w_out}
    _L0_attn_in = _L0_attn_setup()

    def _L0_ffn_setup():
        import jax, jax.numpy as jnp
        import numpy as np
        B, S, H, E = (2, 1024, 128, 8)
        SCALE = 0.5
        key = jax.random.key(seed)
        k1, k2 = jax.random.split(key)
        x = jax.random.normal(k1, (B, S, H), dtype=jnp.float32)
        gate_w = jax.random.normal(k2, (E, H), dtype=jnp.float32) * 0.02
        coeff = SCALE * (1.0 + 0.05 * jnp.arange(E, dtype=jnp.float32))
        expert_w = coeff[:, None, None] * jnp.eye(H, dtype=jnp.float32)
        return {'x': x, 'gate_w': gate_w, 'expert_w': expert_w}
    _L0_ffn_in = _L0_ffn_setup()

    def _L1_attn_setup():
        import jax, jax.numpy as jnp
        import numpy as np
        D_MODEL = 128
        N_HEADS = 16
        WINDOW = 64
        GLOBAL_RATIO = 0.1
        HEAD_DIM = D_MODEL // N_HEADS
        NEG_INF = -1000000000.0
        B, L = (1, 256)
        key = jax.random.key(seed)
        ks = jax.random.split(key, 6)
        x = jax.random.normal(ks[0], (B, L, D_MODEL), jnp.float32)
        s = 1.0 / np.sqrt(D_MODEL)

        def lin(k):
            k1, k2 = jax.random.split(k)
            W = jax.random.uniform(k1, (D_MODEL, D_MODEL), jnp.float32, -s, s)
            b = jax.random.uniform(k2, (D_MODEL,), jnp.float32, -s, s)
            return (W, b)
        Wq, bq = lin(ks[1])
        Wk, bk = lin(ks[2])
        Wv, bv = lin(ks[3])
        Wo, bo = lin(ks[4])
        n_global = max(1, int(L * GLOBAL_RATIO))
        global_indices = jnp.sort(jax.random.randint(ks[5], (n_global,), 0, L))
        return dict(x=x, Wq=Wq, bq=bq, Wk=Wk, bk=bk, Wv=Wv, bv=bv, Wo=Wo, bo=bo, global_indices=global_indices)
    _L1_attn_in = _L1_attn_setup()

    def _L1_ffn_setup():
        import jax, jax.numpy as jnp
        import numpy as np
        NEG_INF = -1e+30

        def _moe_forward(x, router_w, router_b, w1, b1, w2, b2, top_k=2):
            B, S, D = x.shape
            E = router_w.shape[1]
            logits = jnp.einsum('bsd,de->bse', x, router_w) + router_b
            top_vals, top_idx = jax.lax.top_k(logits, top_k)
            keep = jax.nn.one_hot(top_idx, E, dtype=logits.dtype).sum(-2) > 0
            sparse_logits = jnp.where(keep, logits, NEG_INF)
            gating = jax.nn.softmax(sparse_logits, axis=-1)
            xf = x.reshape(-1, D)
            gf = gating.reshape(-1, E)
            h = jax.nn.relu(jnp.einsum('td,edh->eth', xf, w1) + b1[:, None, :])
            y = jnp.einsum('eth,ehd->etd', h, w2) + b2[:, None, :]
            out = jnp.einsum('etd,te->td', y, gf)
            return out.reshape(B, S, D)
        key = jax.random.key(seed)
        ks = jax.random.split(key, 5)
        B, S, D, E, H = (2, 256, 128, 8, 512)
        scale = 0.02
        return {'x': jax.random.normal(ks[0], (B, S, D), dtype=jnp.float32), 'router_w': jax.random.normal(ks[1], (D, E), dtype=jnp.float32) * scale, 'router_b': jnp.zeros((E,), dtype=jnp.float32), 'w1': jax.random.normal(ks[2], (E, D, H), dtype=jnp.float32) * scale, 'b1': jnp.zeros((E, H), dtype=jnp.float32), 'w2': jax.random.normal(ks[3], (E, H, D), dtype=jnp.float32) * scale, 'b2': jnp.zeros((E, D), dtype=jnp.float32)}
    _L1_ffn_in = _L1_ffn_setup()
    _d = {'L0_attn_x': _L0_attn_in['x'], 'L0_attn_w_qkv': _L0_attn_in['w_qkv'], 'L0_attn_w_out': _L0_attn_in['w_out'], 'L0_ffn_gate_w': _L0_ffn_in['gate_w'], 'L0_ffn_expert_w': _L0_ffn_in['expert_w'], 'L1_attn_Wq': _L1_attn_in['Wq'], 'L1_attn_bq': _L1_attn_in['bq'], 'L1_attn_Wk': _L1_attn_in['Wk'], 'L1_attn_bk': _L1_attn_in['bk'], 'L1_attn_Wv': _L1_attn_in['Wv'], 'L1_attn_bv': _L1_attn_in['bv'], 'L1_attn_Wo': _L1_attn_in['Wo'], 'L1_attn_bo': _L1_attn_in['bo'], 'L1_attn_global_indices': _L1_attn_in['global_indices'], 'L1_ffn_router_w': _L1_ffn_in['router_w'], 'L1_ffn_router_b': _L1_ffn_in['router_b'], 'L1_ffn_w1': _L1_ffn_in['w1'], 'L1_ffn_b1': _L1_ffn_in['b1'], 'L1_ffn_w2': _L1_ffn_in['w2'], 'L1_ffn_b2': _L1_ffn_in['b2']}
    _x0 = _d['L0_attn_x']
    _d['L0_attn_x'] = jax.random.normal(jax.random.fold_in(jax.random.key(seed), 1), (16, 256, 128), dtype=_x0.dtype)
    del _x0
    return _d

def reference(L0_attn_x, L0_attn_w_qkv, L0_attn_w_out, L0_ffn_gate_w, L0_ffn_expert_w, L1_attn_Wq, L1_attn_bq, L1_attn_Wk, L1_attn_bk, L1_attn_Wv, L1_attn_bv, L1_attn_Wo, L1_attn_bo, L1_attn_global_indices, L1_ffn_router_w, L1_ffn_router_b, L1_ffn_w1, L1_ffn_b1, L1_ffn_w2, L1_ffn_b2):

    def _L0_attn_ref(x, w_qkv, w_out):
        import jax, jax.numpy as jnp
        import numpy as np
        N_EMBD = 128
        N_HEAD = 16
        HEAD_DIM = N_EMBD // N_HEAD
        ROPE_THETA = 10000.0

        def _rope_cos_sin(seq_len, dim, dtype):
            inv_freq = 1.0 / ROPE_THETA ** (jnp.arange(0, dim, 2, dtype=jnp.float32) / dim)
            ang = jnp.arange(seq_len, dtype=jnp.float32)[:, None] * inv_freq[None, :]
            cos = jnp.concatenate([jnp.cos(ang), jnp.cos(ang)], axis=-1).astype(dtype)
            sin = jnp.concatenate([jnp.sin(ang), jnp.sin(ang)], axis=-1).astype(dtype)
            return (cos, sin)

        def _rotate_half(t):
            d = t.shape[-1] // 2
            return jnp.concatenate([-t[..., d:], t[..., :d]], axis=-1)
        B, S, E = x.shape
        H, D = (N_HEAD, HEAD_DIM)
        qkv = x @ w_qkv
        q, k, v = jnp.split(qkv, 3, axis=-1)
        q = q.reshape(B, S, H, D).transpose(0, 2, 1, 3)
        k = k.reshape(B, S, H, D).transpose(0, 2, 1, 3)
        v = v.reshape(B, S, H, D).transpose(0, 2, 1, 3)
        cos, sin = _rope_cos_sin(S, D, x.dtype)
        q = q * cos + _rotate_half(q) * sin
        k = k * cos + _rotate_half(k) * sin
        scale = 1.0 / np.sqrt(D)
        scores = jnp.einsum('bhqd,bhkd->bhqk', q, k) * scale
        causal = jnp.tril(jnp.ones((S, S), dtype=bool))
        scores = jnp.where(causal[None, None], scores, jnp.float32(-jnp.inf).astype(scores.dtype))
        attn = jax.nn.softmax(scores, axis=-1)
        out = jnp.einsum('bhqk,bhkd->bhqd', attn, v)
        out = out.transpose(0, 2, 1, 3).reshape(B, S, E)
        return out @ w_out

    def _L0_ffn_ref(x, gate_w, expert_w):
        import jax, jax.numpy as jnp
        import numpy as np
        B, S, H, E = (2, 1024, 128, 8)
        SCALE = 0.5
        scores = jnp.einsum('bsh,eh->bse', x, gate_w)
        chosen = jnp.argmax(scores, axis=-1)
        onehot = jax.nn.one_hot(chosen, gate_w.shape[0], dtype=x.dtype)
        expert_out = jnp.einsum('bsh,efh->bsef', x, expert_w)
        return x + jnp.einsum('bsef,bse->bsf', expert_out, onehot)

    def _L1_attn_ref(x, Wq, bq, Wk, bk, Wv, bv, Wo, bo, global_indices):
        import jax, jax.numpy as jnp
        import numpy as np
        D_MODEL = 128
        N_HEADS = 16
        WINDOW = 64
        GLOBAL_RATIO = 0.1
        HEAD_DIM = D_MODEL // N_HEADS
        NEG_INF = -1000000000.0
        B, L = (1, 256)
        Bb, Ll, Dm = x.shape
        H, Dh = (N_HEADS, HEAD_DIM)
        scale = 1.0 / jnp.sqrt(jnp.float32(Dh))
        Q = (x @ Wq.T + bq).reshape(Bb, Ll, H, Dh)
        K = (x @ Wk.T + bk).reshape(Bb, Ll, H, Dh)
        V = (x @ Wv.T + bv).reshape(Bb, Ll, H, Dh)
        half = WINDOW // 2
        W = WINDOW + 1
        pos = jnp.arange(Ll)[:, None] + jnp.arange(-half, half + 1)[None, :]
        valid = (pos >= 0) & (pos < Ll)
        posc = jnp.clip(pos, 0, Ll - 1)
        Kw = K[:, posc]
        Vw = V[:, posc]
        s_loc = jnp.einsum('blhd,blwhd->bhlw', Q, Kw) * scale
        s_loc = jnp.where(valid[None, None], s_loc, NEG_INF)
        a_loc = jax.nn.softmax(s_loc, axis=-1)
        local = jnp.einsum('bhlw,blwhd->blhd', a_loc, Vw)
        Kg = K[:, global_indices]
        Vg = V[:, global_indices]
        s_g = jnp.einsum('blhd,bghd->bhlg', Q, Kg) * scale
        a_g = jax.nn.softmax(s_g, axis=-1)
        glob = jnp.einsum('bhlg,bghd->blhd', a_g, Vg)
        out = 0.7 * local + 0.3 * glob
        return out.reshape(Bb, Ll, Dm) @ Wo.T + bo

    def _L1_ffn_ref(x, router_w, router_b, w1, b1, w2, b2):
        import jax, jax.numpy as jnp
        import numpy as np
        NEG_INF = -1e+30

        def _moe_forward(x, router_w, router_b, w1, b1, w2, b2, top_k=2):
            B, S, D = x.shape
            E = router_w.shape[1]
            logits = jnp.einsum('bsd,de->bse', x, router_w) + router_b
            top_vals, top_idx = jax.lax.top_k(logits, top_k)
            keep = jax.nn.one_hot(top_idx, E, dtype=logits.dtype).sum(-2) > 0
            sparse_logits = jnp.where(keep, logits, NEG_INF)
            gating = jax.nn.softmax(sparse_logits, axis=-1)
            xf = x.reshape(-1, D)
            gf = gating.reshape(-1, E)
            h = jax.nn.relu(jnp.einsum('td,edh->eth', xf, w1) + b1[:, None, :])
            y = jnp.einsum('eth,ehd->etd', h, w2) + b2[:, None, :]
            out = jnp.einsum('etd,te->td', y, gf)
            return out.reshape(B, S, D)
        return _moe_forward(x, router_w, router_b, w1, b1, w2, b2, top_k=2)
    x = L0_attn_x
    x = _layernorm(x + _L0_attn_ref(x, L0_attn_w_qkv, L0_attn_w_out), axis=-1)
    x = _layernorm(x + _L0_ffn_ref(x, L0_ffn_gate_w, L0_ffn_expert_w), axis=-1)
    x = _layernorm(x + _L1_attn_ref(x, L1_attn_Wq, L1_attn_bq, L1_attn_Wk, L1_attn_bk, L1_attn_Wv, L1_attn_bv, L1_attn_Wo, L1_attn_bo, L1_attn_global_indices), axis=-1)
    x = _layernorm(x + _L1_ffn_ref(x, L1_ffn_router_w, L1_ffn_router_b, L1_ffn_w1, L1_ffn_b1, L1_ffn_w2, L1_ffn_b2), axis=-1)
    return x

_drawn_inputs = setup_inputs


def setup_inputs(seed=0):
    import zlib

    import numpy as np

    out = dict(_drawn_inputs(seed))
    spreads = {'L1_ffn_router_b': (0.0, 0.1), 'L1_ffn_b1': (0.0, 0.355), 'L1_ffn_b2': (0.0, 0.1)}
    factors = {'L0_ffn_gate_w': 8.0,
     'L1_attn_Wq': 3.03,
     'L1_attn_bq': 8.0,
     'L1_attn_Wk': 3.084,
     'L1_attn_bk': 8.0}
    for name, (base, spread) in spreads.items():
        noise = np.random.default_rng([zlib.crc32(name.encode()), seed]).standard_normal(out[name].shape)
        drawn = base * np.exp(spread * noise) if base else spread * noise
        out[name] = jnp.asarray(drawn.astype(out[name].dtype))
    for name, factor in factors.items():
        out[name] = (out[name] * factor).astype(out[name].dtype)
    return out
```

```python
from contextlib import ExitStack

import numpy as np

import concourse.bass as bass
from concourse import mybir

F32 = mybir.dt.float32
F32R = mybir.dt.float32r
BF16 = mybir.dt.bfloat16
ALU = mybir.AluOpType
ACT = mybir.ActivationFunctionType
AX = mybir.AxisListType

P = 128
D = 128
S = 256
B = 16
NT = B * S // P
DH = 8
SCALE = float(DH) ** -0.5
EPS = 1e-5
HALF = 32
WIN = P + HALF
NG = 25
NGE = 26
BIG = -1e30
W_LOCAL, W_GLOBAL = 0.7, 0.3


class Attention:

    def __init__(self, name, local, sem):
        self.local = local
        self.units = 4 if local else 3
        self.ring2 = 2 if local else 3
        self.parts = 4 if local else 2
        self.kept = 2 if local else 1

        def s(what):
            return sem(f"{name}_{what}")

        self.x_in = [s("x_in0"), s("x_in1")]
        self.xt_done, self.xt_kept = s("xt_done"), s("xt_kept")
        self.pj_done, self.pj_kept = s("pj_done"), s("pj_kept")
        self.sum_done = s("sum_done")
        self.hi_done, self.ts_done = s("hi_done"), s("ts_done")
        self.sk_done, self.sk_kept = s("sk_done"), s("sk_kept")
        self.p1_done, self.red_done = s("p1_done"), s("red_done")
        self.msp_hi, self.msp_done = s("msp_hi"), s("msp_done")
        self.mx_done, self.mx_kept = s("mx_done"), s("mx_kept")
        self.mrow = [s(f"mrow{j}") for j in range(4)]
        self.p2_done, self.exp_done = s("p2_done"), s("exp_done")
        self.passed = {e: s(f"passed_{e}") for e in ("pe", "dve", "pool")}
        self.masked = s("masked")
        self.vpad = s("vpad")
        self.pv_done, self.ov_kept = s("pv_done"), s("ov_kept")
        self.ot_done, self.rden, self.on_half, self.on_done = s("ot_done"), s("rden"), s("on_half"), s("on_done")
        self.ont_done, self.ot_kept = s("ont_done"), s("ot_kept")
        self.y_done, self.r_done = s("y_done"), s("r_done")
        self.stats, self.aggr = s("stats"), s("aggr")
        self.var_eps, self.rstd, self.x_out = s("var_eps"), s("rstd"), s("x_out")
        if local:
            self.vg_done, self.vg_kept = s("vg_done"), s("vg_kept")
            self.kg_done, self.kg_kept = s("kg_done"), s("kg_kept")
            self.og_half = s("og_half")


class There:

    def __init__(self, i, inner):
        self.vpad = inner or 0 <= i < B
        self.prep = inner or i + 1 < B
        self.scores = inner or 0 <= i < B
        self.late_max = inner or 1 <= i <= B
        self.pv = inner or 1 <= i <= B
        self.finish = inner or 2 <= i <= B + 1
        self.pass2 = [inner or (1 <= i <= B if j < 3 else 0 <= i < B) for j in range(4)]
        self.first = not inner and i <= 0
        self.drain = 0 if inner else max(0, i - B + 1)

    def max_step(self, j):
        return self.late_max if j == 0 else self.scores


def iterations(eng, body):
    for i in (-1, 0, 1):
        body(i, i % 2, There(i, False))
    with eng.Fori(2, B - 3, 2) as i:
        body(i, 0, There(i, True))
        body(i + 1, 1, There(i, True))
    for i in range(B - 2, B + 2):
        body(i, i % 2, There(i, False))


def wait(eng, sem, value):
    if not isinstance(value, int) or value > 0:
        eng.wait_ge(sem, value)


def wait_apart(eng, passed, sem, value):
    if not isinstance(value, int) or value > 0:
        eng.wait_ge(sem, value).then_inc(passed, 1)


def local_items(u):
    return range(3 * u, min(3 * u + 3, 8))


def attention_pe(pe, L, T, W):

    def turn(out, in_):
        return pe.transpose(out, in_, T.ident[:])

    def body(i, p, th):
        n = 1 - p
        fin = i - 2

        def round_ot():
            if th.drain == 0:
                wait(pe, L.sk_kept, 4 * i + 4)
            elif th.drain == 1:
                wait(pe, L.mx_kept, 4 * i - 2)
            else:
                wait(pe, L.ot_kept, i - 2)
            pe.wait_ge(L.ov_kept, L.kept * fin + 1)
            for tau in range(2):
                for r in range(2):
                    m = turn(T.mi[0][:, (2 * tau + r) * P:(2 * tau + r + 1) * P],
                             T.ovs[:, r, tau * P:(tau + 1) * P])
            m.then_inc(L.ot_done, 1)
            if L.local:
                if th.drain == 0:
                    wait(pe, L.kg_kept, i + 1)
                elif th.drain == 1:
                    wait(pe, L.mx_kept, 4 * i - 1)
                else:
                    wait(pe, L.r_done, i - 2)
                pe.wait_ge(L.ov_kept, L.kept * fin + 2)
                for tau in range(2):
                    for r in range(2):
                        m = turn(T.mi[1][:, (2 * tau + r) * P:(2 * tau + r + 1) * P],
                                 T.ogs[:, r, tau * P:(tau + 1) * P])
                m.then_inc(L.ot_done, 1)

        def round_xt():
            if th.finish:
                pe.wait_ge(L.on_done, fin + 1)
            else:
                wait(pe, L.sk_kept, 4 * i + 4)
            pe.wait_ge(L.x_in[n], 8 * (i + 1 - n) + 16)
            if not (isinstance(i, int) and i < 0):
                pe.wait_ge(L.xt_kept, i + 1)
            for tau in range(2):
                m = turn(T.mi[0][:, tau * P:(tau + 1) * P], T.xin[:, n, tau, :])
            m.then_inc(L.xt_done, 1)

        def round_vg():
            if th.finish:
                pe.wait_ge(L.on_done, fin + 1)
            else:
                wait(pe, L.kg_kept, i + 1)
            pe.wait_ge(L.pj_kept, 2 * i + 2)
            for kt in range(2):
                m = pe.matmul(T.mi[1][:, 0:P], T.pick4[:, kt, :], T.vtmp[:, kt, :], start=kt == 0, stop=kt == 1)
            m.then_inc(L.vg_done, 1)

        def round_pj(tau):
            if tau == 0:
                pe.wait_ge(L.xt_kept, i + 2)
            elif th.scores:
                pe.wait_ge(L.mx_kept, 4 * i + 1)
            m = pe.matmul(T.mi[tau][:, 0:3 * D], T.xt[:, tau * P:(tau + 1) * P], W.qkv[:], start=True, stop=True)
            m.then_inc(L.pj_done, 1)

        def round_ont():
            if th.prep:
                pe.wait_ge(L.pj_kept, 2 * i + 3)
            pe.wait_ge(L.on_done, fin + 1)
            for tau in range(2):
                m = turn(T.mi[0][:, tau * P:(tau + 1) * P], T.on[:, tau, :])
            m.then_inc(L.ont_done, 1)

        def round_y():
            if th.prep:
                pe.wait_ge(L.pj_kept, 2 * i + 4)
            elif th.scores:
                pe.wait_ge(L.mx_kept, 4 * i + 1)
            elif th.late_max:
                pe.wait_ge(L.mx_kept, 4 * i)
            wait(pe, L.r_done, fin)
            pe.wait_ge(L.ot_kept, fin + 1)
            for tau in range(2):
                m = pe.matmul(T.mi[1][:, tau * P:(tau + 1) * P], T.ot[:, tau * P:(tau + 1) * P], W.out[:],
                              start=tau == 0, stop=True, skip_group_check=True)
            m.then_inc(L.y_done, 1)

        def round_mx(j):
            step = 4 * i + j - 1
            bank = (1, 1, 0, 1)[j]
            if j == 0:
                if L.local:
                    if th.scores:
                        pe.wait_ge(L.vg_kept, i + 1)
                    else:
                        pe.wait_ge(L.on_done, fin + 1)
                elif th.drain == 0:
                    pe.wait_ge(L.sk_kept, 4 * i + 3)
                else:
                    pe.wait_ge(L.mx_kept, 4 * i - 1)
            elif j == 1:
                if th.late_max:
                    pe.wait_ge(L.mx_kept, 4 * i)
                elif L.local:
                    pe.wait_ge(L.vg_kept, i + 1)
                else:
                    pe.wait_ge(L.sk_kept, 4 * i + 3)
            elif j == 2:
                if th.finish:
                    pe.wait_ge(L.ot_kept, fin + 1)
                else:
                    pe.wait_ge(L.pj_kept, 2 * i + 3)
            else:
                if th.finish:
                    pe.wait_ge(L.r_done, fin + 1)
                else:
                    pe.wait_ge(L.pj_kept, 2 * i + 4)
            pe.wait_ge(L.msp_done, step + 1)
            rows = 4 * L.parts
            for tau in range(2):
                m = turn(T.mi[bank][0:rows, tau * P:(tau + 1) * P], T.msp[:, (j + 1) % 2, tau, 0:rows])
            m.then_inc(L.mx_done, 1)

        def round_sk(k):
            tau, keys = k // 2, k % 2
            bank = (0, 0, 1, 0)[k]
            if k == 0:
                if th.scores:
                    pe.wait_ge(L.mx_kept, 4 * i + 2)
                else:
                    pe.wait_ge(L.pj_kept, 2 * i + 3)
            elif k == 2:
                if th.scores:
                    pe.wait_ge(L.mx_kept, 4 * i + 3)
                else:
                    pe.wait_ge(L.pj_kept, 2 * i + 4)
            else:
                pe.wait_ge(L.sk_kept, 4 * (i + 1) + (1, 2)[k // 2])
            pe.wait_ge(L.ts_done, 2 * (i + 1) + tau + 1)
            for t in range(4):
                m = turn(T.mi[bank][:, t * P:(t + 1) * P], T.ts[:, tau, (4 * keys + t) * P:(4 * keys + t + 1) * P])
            m.then_inc(L.sk_done, 1)

        def round_kg():
            pe.wait_ge(L.sk_kept, 4 * (i + 1) + 3)
            pe.wait_ge(L.ts_done, 2 * (i + 1) + 2)
            for t in range(4):
                for kt in range(2):
                    m = pe.matmul(T.mi[1][:, t * 32:t * 32 + NGE], T.tsr[:, kt, (4 + t) * P:(5 + t) * P],
                                  T.pick[:, kt, :], start=t == 0 and kt == 0, stop=kt == 1, skip_group_check=True)
            m.then_inc(L.kg_done, 1)

        def pass1(j, u):
            unit = L.units * (4 * i + j) + u
            bank = T.s1[u % 2 if L.local else (j + u) % 2]
            if u == 0 and j == 0:
                pe.wait_ge(L.sk_kept, 4 * i + 4)
                if L.local:
                    pe.wait_ge(L.kg_kept, i + 1)
            wait(pe, L.red_done, unit - 1)
            q, k = T.qs[p], T.ks[p]
            rows = slice(32 * j, 32 * j + 24)
            if L.local and u == 3:
                for item in range(8):
                    tau, t = divmod(item, 4)
                    m = pe.matmul(bank[:, item * NGE:(item + 1) * NGE], q[rows, t, tau * P:(tau + 1) * P],
                                  T.kg[p][rows, t, 0:NGE], start=item == 0, stop=True, skip_group_check=True)
            elif L.local:
                items = local_items(u)
                cols = len(items) * WIN
                pe.matmul(bank[:, 0:cols], T.identb[:], T.band[:, 3 * u * WIN:3 * u * WIN + cols],
                          start=True, stop=False, skip_group_check=True)
                for c, item in enumerate(items):
                    tau, t = divmod(item, 4)
                    lo = tau * (S - WIN)
                    m = pe.matmul(bank[:, c * WIN:(c + 1) * WIN], q[rows, t, tau * P:(tau + 1) * P],
                                  k[rows, t, lo:lo + WIN], start=False, stop=True, skip_group_check=True)
            elif u == 0:
                pe.matmul(bank[:, :], T.identb[:], T.causal[:, :], start=True, stop=False, skip_group_check=True)
                for t in range(4):
                    m = pe.matmul(bank[:, t * P:(t + 1) * P], q[rows, t, 0:P], k[rows, t, 0:P],
                                  start=False, stop=True, skip_group_check=True)
            else:
                for c in range(2):
                    pe.matmul(bank[:, c * S + P:(c + 1) * S], T.identb[:], T.causal[:, 0:P],
                              start=c == 0, stop=False, skip_group_check=True)
                for c in range(2):
                    t = 2 * (u - 1) + c
                    m = pe.matmul(bank[:, c * S:(c + 1) * S], q[rows, t, P:S], k[rows, t, :],
                                  start=False, stop=True, skip_group_check=True)
            m.then_inc(L.p1_done, 1)

        def pass2(j, u):
            js = (j + 1) % 4
            par, batch = (n, i - 1) if j < 3 else (p, i)
            unit = L.units * (4 * i + j - 3) + u
            bank = T.s2[u % 2] if L.local else T.s2[u]
            if u == 0:
                pe.wait_ge(L.mrow[js], 64 * batch + 64)
            wait_apart(pe, L.passed["pe"], L.exp_done, unit - L.ring2 + 1)
            q, k = T.qs[par], T.ks[par]
            rows = slice(32 * js, 32 * js + 26)
            if L.local and u == 3:
                rows = slice(32 * js, 32 * js + 28)
                for t in range(4):
                    m = pe.matmul(bank[32 * t:32 * t + 32, 0:S], T.kg[par][rows, t, :].bitcast(F32),
                                  q[rows, t, :].bitcast(F32), start=True, stop=True)
            elif L.local:
                items = local_items(u)
                cols = len(items) * WIN
                pe.matmul(bank[:, 0:cols], T.identb[:], T.band[:, 3 * u * WIN:3 * u * WIN + cols],
                          start=True, stop=False, skip_group_check=True)
                for c, item in enumerate(items):
                    kt, t = divmod(item, 4)
                    lo = kt * (S - WIN)
                    m = pe.matmul(bank[:, c * WIN:(c + 1) * WIN], k[rows, t, kt * P:(kt + 1) * P],
                                  q[rows, t, lo:lo + WIN], start=False, stop=True, skip_group_check=True)
            elif u == 0:
                for t in range(4):
                    m = pe.matmul(bank[:, t * P:(t + 1) * P], k[rows, t, P:S], q[rows, t, P:S],
                                  start=t == 0, stop=True, skip_group_check=True)
            else:
                for c in range(2):
                    t = 2 * (u - 1) + c
                    m = pe.matmul(bank[:, c * S:(c + 1) * S], k[rows, t, 0:P], q[rows, t, :],
                                  start=c == 0, stop=True, skip_group_check=True)
            m.then_inc(L.p2_done, 1)

        def pv(j):
            step = 4 * (i - 1) + j
            pb = T.p[j % 2]
            r = j // 2
            if j == 0:
                pe.wait_ge(L.vpad, i)
                if L.local:
                    pe.wait_ge(L.vg_kept, i)
                wait(pe, L.ov_kept, L.kept * (i - 1))
            if L.local:
                pe.wait_ge(L.exp_done, 4 * step + 4)
                for item in range(8):
                    kt, t = divmod(item, 4)
                    lo = r * S + kt * (S - WIN)
                    pe.matmul(T.ov[32 * t:32 * t + 32, lo:lo + WIN], T.vb[n][:, kt, j, t, :],
                              pb[:, item // 3, item % 3 * WIN:(item % 3 + 1) * WIN],
                              start=j == 0 and kt == 0, stop=False, skip_group_check=True)
                m = pe.matmul(T.og[:, r * S:(r + 1) * S], T.vgb[n][:, j, :], pb[:, 3, 0:S],
                              start=j == 0, stop=False, skip_group_check=True)
            else:
                pe.wait_ge(L.masked, 3 * step + 3)
                for t in range(4):
                    pe.matmul(T.ov[32 * t:32 * t + 32, r * S:(r + 1) * S], T.vb[n][:, 0, j, t, :],
                              pb[:, 1 + t // 2, t % 2 * S:(t % 2 + 1) * S],
                              start=j == 0, stop=False, skip_group_check=True)
                for t in range(4):
                    m = pe.matmul(T.ov[32 * t:32 * t + 32, r * S + P:(r + 1) * S], T.vb[n][:, 1, j, t, :],
                                  pb[:, 0, t * P:(t + 1) * P],
                                  start=False, stop=False, skip_group_check=True)
            m.then_inc(L.pv_done, 1)

        for j in range(4):
            for u in range(L.units):
                if th.scores:
                    pass1(j, u)
                if j == 0 and u == 0 and th.finish:
                    round_ot()
                if j == 0 and u == 1:
                    if th.prep:
                        round_xt()
                    if L.local and th.scores:
                        round_vg()
                if j == 0 and u == 2 and th.late_max:
                    round_mx(0)
                if j in (1, 2) and u == 0 and th.prep:
                    round_pj(j - 1)
                if j > 0 and u == 1 and th.scores:
                    round_mx(j)
                if j == 1 and u == 2 and th.finish:
                    round_ont()
                if j == 2 and u == 2 and th.finish:
                    round_y()
                if j == 3 and u in (0, 2) and th.prep:
                    round_sk(u // 2)
                if th.pass2[j]:
                    pass2(j, u)
            if j == 3 and th.prep:
                round_sk(2)
                round_sk(3)
                if L.local:
                    round_kg()
            if th.pv:
                pv(j)

    iterations(pe, body)


def attention_act(act, L, T, W):

    def body(i, p, th):
        n = 1 - p
        fin = i - 2

        def keep_pv():
            act.wait_ge(L.pv_done, 4 * fin + 4)
            if not (isinstance(i, int) and i == 2):
                act.wait_ge(L.ot_done, L.kept * fin)
            act.copy(T.ovs[:, :, :], T.ov[:, :].rearrange("p (r q) -> p r q", r=2)).then_inc(L.ov_kept, 1)
            if L.local:
                act.copy(T.ogs[:, :, :], T.og[:, :].rearrange("p (r q) -> p r q", r=2)).then_inc(L.ov_kept, 1)

        def keep_xt():
            act.wait_ge(L.xt_done, i + 2)
            wait(act, L.pj_done, 2 * i + 2)
            act.copy(T.xt[:, :], T.mi[0][:, 0:S]).then_inc(L.xt_kept, 1)

        def keep_mx(j):
            bank = (1, 1, 0, 1)[j]
            js = (j + 3) % 4
            batch = i - 1 if j == 0 else i
            act.wait_ge(L.mx_done, 4 * i + j)
            wait(act, L.mrow[js], 64 * batch)
            rows = 4 * L.parts
            act.copy(T.mt[js][0:rows, :], T.mi[bank][0:rows, 0:S]).then_inc(L.mx_kept, 1)

        def split_hi(tau):
            act.wait_ge(L.sum_done, 2 * (i + 1) + tau + 1)
            wait(act, L.sk_done, 4 * (i + 1))
            if L.local:
                wait(act, L.kg_done, i + 1)
            ts = T.tsr[:, tau, :].rearrange("p (h c d) -> p h c d", h=32, d=DH)
            rq = T.rq[:, tau, :].rearrange("p (h o d) -> p h o d", h=32, o=1)
            act.copy(ts[:, 0:16, 0:3:2, :], rq[:, 0:16].to_broadcast([P, 16, 2, DH]))
            act.copy(ts[:, 16:32, 0:2, :], rq[:, 16:32].to_broadcast([P, 16, 2, DH])).then_inc(L.hi_done, 1)

        def keep_ot():
            act.wait_ge(L.ont_done, fin + 1)
            wait(act, L.y_done, fin)
            act.copy(T.ot[:, :], T.mi[0][:, 0:S]).then_inc(L.ot_kept, 1)

        def keep_sk(k):
            tau, keys = k // 2, k % 2
            bank = (0, 0, 1, 0)[k]
            act.wait_ge(L.sk_done, 4 * (i + 1) + k + 1)
            out = (T.ks if keys else T.qs)[n]
            act.copy(out[:, :, tau * P:(tau + 1) * P],
                     T.mi[bank][:, :].rearrange("p (t q) -> p t q", t=4)).then_inc(L.sk_kept, 1)

        def keep_kg():
            act.wait_ge(L.kg_done, i + 2)
            act.copy(T.kg[n][:, :, 0:NGE],
                     T.mi[1][:, 0:4 * 32].rearrange("p (t g) -> p t g", t=4)[:, :, 0:NGE]).then_inc(L.kg_kept, 1)

        def exp(j, u):
            step = 4 * i + j - 3
            pb = T.p[(j + 1) % 2]
            bank = T.s2[u % 2] if L.local else T.s2[u]
            cols = (S if u == 3 else len(local_items(u)) * WIN) if L.local else 512
            act.wait_ge(L.p2_done, L.units * step + u + 1)
            if u == 0:
                wait(act, L.pv_done, step - 1)
            act.activation(pb[:, u, 0:cols], bank[:, 0:cols], ACT.Exp, scale=SCALE).then_inc(L.exp_done, 1)

        for j in range(4):
            if j == 0 and th.finish:
                keep_pv()
            for u in range(L.units):
                if j == 0 and u == 1 and th.prep:
                    keep_xt()
                if (j == 0 and u == 2 or j > 0 and u == 1) and th.max_step(j):
                    keep_mx(j)
                if j == 1 and u == 2 and th.finish:
                    keep_ot()
                if j == 3 and u in (0, 2) and th.prep:
                    keep_sk(u // 2)
                if th.pass2[j]:
                    exp(j, u)
            if j in (1, 2) and th.prep:
                split_hi(j - 1)
            if j == 3 and th.prep:
                keep_sk(2)
                keep_sk(3)
                if L.local:
                    keep_kg()

    iterations(act, body)


def attention_dve(dve, L, T, W):

    def body(i, p, th):
        n = 1 - p
        fin = i - 2

        def normalise():
            heads = T.mi[0][:, :].rearrange("p (h c) -> p h c", c=16)
            on = T.on[:, :, :].rearrange("p a (h d) -> p (a h) d", d=DH)
            dve.wait_ge(L.ot_done, L.kept * fin + 1)
            wait(dve, L.ont_done, fin)
            if not L.local:
                dve.reciprocal(T.rd[:, 0, :], heads[:, :, DH]).then_inc(L.rden, 1)
                dve.wait_ge(L.rden, fin + 1)
                dve.tensor_tensor(on, heads[:, :, 0:DH],
                                  T.rd[:, 0, :].rearrange("p (h o) -> p h o", o=1).to_broadcast([P, 32, DH]),
                                  ALU.mult).then_inc(L.on_done, 1)
                return
            glob = T.mi[1][:, :].rearrange("p (h c) -> p h c", c=16)
            ong = T.ong[:, :].rearrange("p (h d) -> p h d", d=DH)
            dve.reciprocal(T.rd[:, 0, :], heads[:, :, DH]).then_inc(L.rden, 1)
            dve.wait_ge(L.ot_done, L.kept * fin + 2)
            dve.reciprocal(T.rd[:, 1, :], glob[:, :, DH]).then_inc(L.rden, 1)
            dve.wait_ge(L.rden, 2 * fin + 1)
            dve.tensor_tensor(on, heads[:, :, 0:DH],
                              T.rd[:, 0, :].rearrange("p (h o) -> p h o", o=1).to_broadcast([P, 32, DH]),
                              ALU.mult).then_inc(L.on_half, 1)
            dve.wait_ge(L.rden, 2 * fin + 2)
            dve.tensor_tensor(ong, glob[:, :, 0:DH],
                              T.rd[:, 1, :].rearrange("p (h o) -> p h o", o=1).to_broadcast([P, 32, DH]),
                              ALU.mult).then_inc(L.og_half, 1)
            dve.wait_ge(L.on_half, fin + 1)
            dve.wait_ge(L.og_half, fin + 1)
            dve.tensor_tensor(on, on, ong, ALU.add).then_inc(L.on_done, 1)

        def keep_vg():
            dve.wait_ge(L.vg_done, i + 1)
            wait(dve, L.pv_done, 4 * (i - 1))
            vg = T.mi[1][:, 0:D].rearrange("p (t r s d) -> p r s t d", t=4, r=2, s=2)
            out = T.vgb[p][:, :, :].rearrange("p (r s) (t z c) -> p r s t z c", r=2, t=4, z=2)
            mask = T.diag[:, :].rearrange("p (t d) -> p t d", t=4)
            for s in range(2):
                for r in range(2):
                    m = dve.tensor_tensor(out[:, r, s, :, s, 0:DH], vg[:, r, s, :, :], mask, ALU.mult)
            m.then_inc(L.vg_kept, 1)

        def keep_pj(tau):
            dve.wait_ge(L.pj_done, 2 * (i + 1) + tau + 1)
            wait(dve, L.ts_done, 2 * i + tau + 1)
            mi = T.mi[tau]
            if not L.local:
                qk = mi[:, 0:2 * D].rearrange("p (h a f) -> p h a f", h=32, a=2)
                rs = T.rs[:, tau, :].rearrange("p (h a f) -> p h a f", h=32, a=2)
                cos = T.cos[:, tau, :].rearrange("p (o d) -> p o d", o=1)
                sin = T.sin[:, tau, :].rearrange("p (o a f) -> p o a f", o=1, a=2)
                dve.tensor_tensor(T.rq[:, tau, :].rearrange("p (h d) -> p h d", h=32),
                                  mi[:, 0:2 * D].rearrange("p (h d) -> p h d", h=32),
                                  cos.to_broadcast([P, 32, DH]), ALU.mult)
                dve.tensor_tensor(rs, qk[:, :, ::-1, :], sin.to_broadcast([P, 32, 2, DH // 2]), ALU.mult)
            else:
                dve.tensor_tensor(T.rq[:, tau, :], mi[:, 0:2 * D], W.bqkv[:, 0:2 * D], ALU.add).then_inc(L.sum_done, 1)
            wait(dve, L.vpad, i + 1)
            if L.local:
                wait(dve, L.vg_done, i + 1)
                dve.tensor_tensor(T.vtmp[:, tau, :], mi[:, 2 * D:3 * D], W.bqkv[:, 2 * D:3 * D],
                                  ALU.add).then_inc(L.pj_kept, 1)
            else:
                dve.tensor_copy(T.vtmp[:, tau, :], mi[:, 2 * D:3 * D]).then_inc(L.pj_kept, 1)

        def maxima(j, u):
            step = 4 * i + j
            bank = T.s1[u % 2 if L.local else (j + u) % 2]
            dve.wait_ge(L.p1_done, L.units * step + u + 1)
            if u == 0:
                wait(dve, L.msp_done, step - 1)
            nm = T.nm[:, j % 2, 0, :]
            if L.local and u == 3:
                src = bank[:, 0:8 * NGE].rearrange("p (h k) -> p h k", k=NGE)[:, :, 0:NG]
                out = T.nm[:, j % 2, 1, :]
            elif L.local:
                items = local_items(u)
                src = bank[:, 0:len(items) * WIN].rearrange("p (h k) -> p h k", k=WIN)
                out = nm[:, items[0]:items[-1] + 1]
            elif u == 0:
                src, out = bank[:, :].rearrange("p (h k) -> p h k", h=4), nm[:, 0:4]
            else:
                src, out = bank[:, :].rearrange("p (h k) -> p h k", h=2), nm[:, 2 + 2 * u:4 + 2 * u]
            dve.tensor_reduce(out, src, AX.X, ALU.max, negate=True).then_inc(L.red_done, 1)

        def residual():
            dve.wait_ge(L.y_done, fin + 1)
            wait(dve, L.x_out, 2 * fin)
            dve.tensor_tensor(T.r[:, :, :], T.mi[1][:, 0:S].rearrange("p (a d) -> p a d", a=2),
                              W.resid[:, bass.ds(2 * fin, 2), :], ALU.add).then_inc(L.r_done, 1)
            dve.wait_ge(L.r_done, fin + 1)
            wait(dve, L.aggr, 2 * fin)
            for tau in range(2):
                dve.bn_stats(T.st[:, tau, :], T.r[:, tau, :]).then_inc(L.stats, 1)
            wait(dve, L.rstd, fin)
            for tau in range(2):
                wait_apart(dve, L.passed["dve"], L.stats, 2 * fin + tau + 1)
                dve.bn_aggr(T.mv[:, tau, :], T.st[:, tau, :]).then_inc(L.aggr, 1)

        def layernorm():
            dve.wait_ge(L.rstd, fin + 1)
            for tau in range(2):
                dve.tensor_scalar(W.x_next[:, bass.ds(2 * fin + tau, 1), :], T.r[:, tau:tau + 1, :],
                                  T.mv[:, tau, 0:1], T.rs2[:, tau:tau + 1],
                                  ALU.subtract, ALU.mult).then_inc(L.x_out, 1)

        for j in range(4):
            for u in range(L.units):
                if j == 0 and u == 1 and th.finish:
                    normalise()
                if L.local and j == 0 and u == 2 and th.scores:
                    keep_vg()
                if j in (1, 2) and u == 1 and th.prep:
                    keep_pj(j - 1)
                if j == 3 and u == 0 and th.finish:
                    residual()
                if th.scores:
                    maxima(j, u)
            if j == 3 and th.finish:
                layernorm()

    iterations(dve, body)


def attention_pool(pool, L, T, W):

    def body(i, p, th):
        fin = i - 2

        def lay_out_v():
            wait_apart(pool, L.passed["pool"], L.pj_kept, 2 * i + 2)
            wait_apart(pool, L.passed["pool"], L.pv_done, 4 * (i - 1))
            v = T.vtmp[:, :, :].rearrange("p k (t r s d) -> p k s r t d", t=4, r=2, s=2)
            out = T.vb[p][:, :, :, :, :].rearrange("p k (r s) t (z c) -> p k s r t z c", r=2, z=2)
            for kt in range(2):
                for s in range(2):
                    m = pool.tensor_copy(out[:, kt, s, :, :, s, 0:DH], v[:, kt, s])
            m.then_inc(L.vpad, 1)

        def split_maxima(j):
            step = 4 * i + j - 1
            js = (j + 1) % 2
            wait_apart(pool, L.passed["pool"], L.red_done, L.units * (step + 1))
            wait_apart(pool, L.passed["pool"], L.mx_done, step - 1)
            nm = T.nm[:, js, :, :].rearrange("p g (a t) -> p g a t", a=2)
            msp = T.msp[:, js, :, 0:4 * L.parts].rearrange("p a (t c) -> p a t c", t=4)
            mspr = T.mspr[:, js, :, 0:4 * L.parts].rearrange("p a (t c) -> p a t c", t=4)
            if L.local:
                dm = T.dm[:, :].rearrange("p (a t) -> p a t", a=2)
                pool.tensor_tensor(dm, nm[:, 1], nm[:, 0], ALU.subtract).then_inc(L.msp_hi, 1)
            pool.tensor_copy(mspr[:, :, :, 0], nm[:, 0]).then_inc(L.msp_hi, 1)
            if L.local:
                wait_apart(pool, L.passed["pool"], L.msp_hi, 3 * step + 1)
                pool.tensor_copy(mspr[:, :, :, 2], dm).then_inc(L.msp_hi, 1)
                pool.wait_ge(L.msp_hi, 3 * step + 3)
                pool.tensor_tensor(mspr[:, :, :, 3], dm, msp[:, :, :, 2], ALU.subtract)
            else:
                pool.wait_ge(L.msp_hi, step + 1)
            pool.tensor_tensor(mspr[:, :, :, 1], nm[:, 0], msp[:, :, :, 0], ALU.subtract).then_inc(L.msp_done, 1)

        def add_rotated(tau):
            pool.wait_ge(L.pj_kept, 2 * (i + 1) + tau + 1)
            pool.tensor_tensor(T.rq[:, tau, :], T.rq[:, tau, :], T.rs[:, tau, :], ALU.add).then_inc(L.sum_done, 1)

        def split_lo(tau):
            pool.wait_ge(L.hi_done, 2 * (i + 1) + tau + 1)
            ts = T.ts[:, tau, :].rearrange("p (h c d) -> p h c d", h=32, d=DH)
            tsr = T.tsr[:, tau, :].rearrange("p (h c d) -> p h c d", h=32, d=DH)
            rq = T.rq[:, tau, :].rearrange("p (h d) -> p h d", h=32)
            pool.tensor_tensor(tsr[:, 0:16, 1, :], rq[:, 0:16], ts[:, 0:16, 0, :], ALU.subtract)
            pool.tensor_tensor(tsr[:, 16:32, 2, :], rq[:, 16:32], ts[:, 16:32, 0, :],
                               ALU.subtract).then_inc(L.ts_done, 1)

        def mask(j, u):
            step = 4 * i + j - 3
            pb = T.p[(j + 1) % 2][:, u, :]
            wait_apart(pool, L.passed["pool"], L.exp_done, 3 * step + u + 1)
            heads = 4 if u == 0 else 2
            at = pb.rearrange("p (h q) -> p h q", h=heads)[:, :, 0:P]
            pool.affine_select(out=at, in_=at, compare_op=ALU.is_ge, fill=0.0, base=0,
                               pattern=[[0, heads], [1, P]], channel_multiplier=-1).then_inc(L.masked, 1)

        def inverse_deviation():
            wait_apart(pool, L.passed["pool"], L.aggr, 2 * fin + 2)
            wait_apart(pool, L.passed["pool"], L.x_out, 2 * fin)
            pool.tensor_scalar(T.ve[:, :], T.mv[:, :, 1], EPS, None, ALU.add).then_inc(L.var_eps, 1)
            pool.wait_ge(L.var_eps, fin + 1)
            pool.tensor_tensor(T.rs2[:, :], T.ve[:, :], T.mhalf[:, 0:2], ALU.pow).then_inc(L.rstd, 1)

        for j in range(4):
            if th.max_step(j):
                split_maxima(j)
            if j == 0 and th.vpad:
                lay_out_v()
            if j > 1 and th.prep:
                split_lo(j - 2)
            if j in (1, 2) and th.prep and not L.local:
                add_rotated(j - 1)
            if not L.local and th.pass2[j]:
                for u in range(3):
                    mask(j, u)
            if j == 3 and th.finish:
                inverse_deviation()

    iterations(pool, body)


def attention_sp(sp, L, T, W):

    def body(i, p, th):
        def load(batch, par):
            sp.dma_start(T.xin[:, par, :, :], W.x_batch(batch)).then_inc(L.x_in[par], 16)

        if isinstance(i, int) and i == -1:
            load(0, 0)
            load(1, 1)
            return
        if not isinstance(i, int) or i + 2 < B:
            sp.wait_ge(L.xt_done, i + 1)
            load(i + 2, p)
        for j in range(4):
            if not th.max_step(j):
                continue
            js = (j + 3) % 4
            q = T.qs[(1 - p) if j == 0 else p]
            sp.wait_ge(L.mx_kept, 4 * i + j)
            for t in range(4):
                sp.dma_start(q[32 * js + 24:32 * js + 24 + L.parts, t, :].bitcast(F32),
                             T.mt[js][L.parts * t:L.parts * (t + 1), :].bitcast(F32)).then_inc(L.mrow[js], 16)

    iterations(sp, body)


E = 8
HID = 512
HC = HID // P
G4 = 4
GROUPS = NT // G4


class Mixture:

    def __init__(self, name, steps, per_tile, sem):
        self.steps = steps
        self.per_tile = per_tile

        def s(what):
            return sem(f"{name}_{what}")

        self.xf_in = [s("xf_in0"), s("xf_in1")]
        self.ft_done, self.ft_kept = s("ft_done"), s("ft_kept")
        self.gate_done, self.gate_read = s("gate_done"), s("gate_read")
        self.route = s("route")
        self.y_done, self.acc = s("y_done"), s("acc")
        self.stats, self.aggr, self.var_eps = s("stats"), s("aggr"), s("var_eps")
        self.rstd, self.x_out = s("rstd"), s("x_out")
        self.passed = {e: s(f"passed_{e}") for e in ("dve", "pool")}
        if steps > 5:
            self.exp_done = s("exp_done")
            self.gt_done, self.gt_kept = s("gt_done"), s("gt_kept")
            self.b2_done = s("b2_done")
            self.h_done, self.relu_done = s("h_done"), s("relu_done")


def groups(eng, body):
    for g in range(2):
        body(g, g)
    with eng.Fori(2, GROUPS - 1, 2) as g:
        body(g, 0)
        body(g + 1, 1)


def mixture_sp(sp, M, T, x_from):

    def body(g, p):
        wait(sp, M.acc, M.per_tile * G4 * (g - 1))
        sp.dma_start(T.xf[p][:, :, :], x_from[:, bass.ds(G4 * g, G4), :]).then_inc(M.xf_in[p], 16)

    groups(sp, body)


def turn_tokens(pe, M, T, g, p):
    pe.wait_ge(M.xf_in[p], 8 * (g - p) + 16)
    wait(pe, M.ft_kept, g)
    for a in range(G4):
        m = pe.transpose(T.mi[0][:, a * P:(a + 1) * P], T.xf[p][:, a, :], T.ident[:])
    m.then_inc(M.ft_done, 1)


def gate(pe, M, T, g, p, w):
    pe.wait_ge(M.ft_kept, g + 1)
    wait(pe, M.gate_read, g)
    for a in range(G4):
        m = pe.matmul(T.mi[1][:, a * E:(a + 1) * E], T.xt4[p][:, a * P:(a + 1) * P], w,
                      start=a == 0, stop=True, skip_group_check=True)
    m.then_inc(M.gate_done, 1)


def layernorm_group(dve, M, T, g, x_to):
    wait(dve, M.aggr, G4 * g)
    dve.wait_ge(M.acc, M.per_tile * G4 * (g + 1))
    for a in range(G4):
        dve.bn_stats(T.st4[:, a, :], T.sum[:, a, :]).then_inc(M.stats, 1)
    wait(dve, M.rstd, g)
    for a in range(G4):
        wait_apart(dve, M.passed["dve"], M.stats, G4 * g + a + 1)
        dve.bn_aggr(T.mv4[:, a, :], T.st4[:, a, :]).then_inc(M.aggr, 1)
    dve.wait_ge(M.rstd, g + 1)
    for a in range(G4):
        dve.tensor_scalar(x_to[:, bass.ds(G4 * g + a, 1), :], T.sum[:, a:a + 1, :],
                          T.mv4[:, a, 0:1], T.rs4[:, a:a + 1], ALU.subtract, ALU.mult).then_inc(M.x_out, 1)


def mixture_pool(pool, M, T):

    def body(g, p):
        wait_apart(pool, M.passed["pool"], M.aggr, G4 * (g + 1))
        wait_apart(pool, M.passed["pool"], M.x_out, G4 * g)
        pool.tensor_scalar(T.ve4[:, :], T.mv4[:, :, 1], EPS, None, ALU.add).then_inc(M.var_eps, 1)
        pool.wait_ge(M.var_eps, g + 1)
        pool.tensor_tensor(T.rs4[:, :], T.ve4[:, :], T.mhalf[:, :], ALU.pow).then_inc(M.rstd, 1)

    groups(pool, body)


def spread(column, width):
    n = column.shape[1]
    return column.rearrange("p (a o) -> p a o", o=1).to_broadcast([P, n, width])


def choose(dve, M, T, scores, best, chosen, at):
    dve.tensor_reduce(best, scores, AX.X, ALU.max).then_inc(M.route, 1)
    dve.wait_ge(M.route, at + 1)
    dve.tensor_tensor(T.eq[:, :, :], scores, spread(best, E), ALU.is_ge).then_inc(M.route, 1)
    dve.wait_ge(M.route, at + 2)
    dve.tensor_tensor(T.rank[:, :, :], T.eq[:, :, :], T.first[:, :].rearrange("p (a e) -> p a e", e=E),
                      ALU.mult).then_inc(M.route, 1)
    dve.wait_ge(M.route, at + 3)
    dve.tensor_reduce(T.top[:, :], T.rank[:, :, :], AX.X, ALU.max).then_inc(M.route, 1)
    dve.wait_ge(M.route, at + 4)
    dve.tensor_tensor(chosen, T.rank[:, :, :], spread(T.top[:, :], E), ALU.is_equal).then_inc(M.route, 1)
    dve.wait_ge(M.route, at + 5)


def one_expert_pe(pe, M, T, W):

    def body(g, p):
        turn_tokens(pe, M, T, g, p)
        gate(pe, M, T, g, p, W.gate[:])
        for a in range(G4):
            for half in range(2):
                if half == 0:
                    wait(pe, M.acc, M.per_tile * (G4 * g + a - 1))
                m = pe.matmul(T.y2[a % 2][half][:, :], T.xt4[p][:, a * P:(a + 1) * P],
                              W.expert[:, half * 512:(half + 1) * 512], start=True, stop=True)
            m.then_inc(M.y_done, 1)

    groups(pe, body)


def one_expert_act(act, M, T):
    def body(g, p):
        act.wait_ge(M.ft_done, g + 1)
        wait(act, M.y_done, G4 * (g - 1))
        act.copy(T.xt4[p][:, :], T.mi[0][:, :]).then_inc(M.ft_kept, 1)

    groups(act, body)


def one_expert_dve(dve, M, T, x_to):

    def body(g, p):
        dve.wait_ge(M.gate_done, g + 1)
        at = 5 * g
        scores = T.mi[1][:, 0:G4 * E].rearrange("p (a e) -> p a e", e=E)
        wait(dve, M.acc, M.per_tile * G4 * g)
        choose(dve, M, T, scores, T.best[:, :], T.gates[:, :, :], at)
        dve.tensor_copy(T.top[:, :], T.best[:, :]).then_inc(M.gate_read, 1)
        wait(dve, M.x_out, G4 * g)
        for a in range(G4):
            n = M.per_tile * (G4 * g + a)
            dve.wait_ge(M.y_done, G4 * g + a + 1)
            for e in range(E):
                if e:
                    dve.wait_ge(M.acc, n + e)
                dve.scalar_tensor_tensor(T.sum[:, a, :], T.y2[a % 2][e // 4][:, (e % 4) * P:(e % 4 + 1) * P],
                                         T.gates[:, a, e:e + 1], T.sum[:, a, :] if e else T.xf[p][:, a, :],
                                         ALU.mult, ALU.add).then_inc(M.acc, 1)
            dve.wait_ge(M.acc, n + E)
            dve.tensor_tensor(T.sum[:, a, :], T.sum[:, a, :], T.xf[p][:, a, :], ALU.add).then_inc(M.acc, 1)
        layernorm_group(dve, M, T, g, x_to)

    groups(dve, body)


def two_experts_pe(pe, M, T, W):

    def body(g, p):
        turn_tokens(pe, M, T, g, p)
        gate(pe, M, T, g, p, W.router[:])
        pe.wait_ge(M.route, M.steps * (g + 1))
        for a in range(G4):
            m = pe.transpose(T.mi[1][0:E, a * P:(a + 1) * P], T.gates[:, a, :], T.ident[:])
        m.then_inc(M.gt_done, 1)
        pe.wait_ge(M.gt_kept, g + 1)
        for a in range(G4):
            m = pe.matmul(T.mi[1][:, a * P:(a + 1) * P], T.gt[:, a * P:(a + 1) * P], W.b2[:],
                          start=a == 0, stop=True, skip_group_check=True)
        m.then_inc(M.b2_done, 1)

        def hidden(n):
            e, c = divmod(n, HC)
            wait(pe, M.relu_done, E * HC * g + n - 1)
            pe.matmul(T.hb[n % 2][:, :], W.w1[:, e, c * P:(c + 1) * P], T.xt4[p][:, :],
                      start=True, stop=True).then_inc(M.h_done, 1)

        hidden(0)
        for n in range(E * HC):
            if n + 1 < E * HC:
                hidden(n + 1)
            e, c = divmod(n, HC)
            if c == 0:
                wait(pe, M.acc, G4 * ((E + 1) * g + e))
            pe.wait_ge(M.relu_done, E * HC * g + n + 1)
            for a in range(G4):
                m = pe.matmul(T.yb[e % 2][:, a * P:(a + 1) * P], T.h[n % 4][:, a * P:(a + 1) * P], W.w2[:, e, c, :],
                              start=c == 0 and a == 0, stop=c == HC - 1, skip_group_check=True)
            m.then_inc(M.y_done, 1)

    groups(pe, body)


def two_experts_act(act, M, T, W):

    def body(g, p):
        act.wait_ge(M.ft_done, g + 1)
        wait(act, M.y_done, E * HC * (g - 1))
        act.copy(T.xt4[p][:, :], T.mi[0][:, :]).then_inc(M.ft_kept, 1)
        act.wait_ge(M.route, M.steps * g + 12)
        act.activation(T.e2[:, :], T.diff[:, :], ACT.Exp).then_inc(M.exp_done, 1)
        act.wait_ge(M.gt_done, g + 1)
        act.copy(T.gt[:, :], T.mi[1][0:E, :]).then_inc(M.gt_kept, 1)
        for n in range(E * HC):
            act.wait_ge(M.h_done, E * HC * g + n + 1)
            wait(act, M.y_done, E * HC * g + n - 3)
            act.activation(T.h[n % 4][:, :], T.hb[n % 2][:, :], ACT.Relu,
                           bias=W.b1[:, n:n + 1]).then_inc(M.relu_done, 1)

    groups(act, body)


def two_experts_dve(dve, M, T, W, x_to):

    def body(g, p):
        at = M.steps * g
        wait(dve, M.acc, (E + 1) * G4 * g)
        dve.wait_ge(M.gate_done, g + 1)
        dve.tensor_tensor(T.logits[:, :, :], T.mi[1][:, 0:G4 * E].rearrange("p (a e) -> p a e", e=E),
                          W.rb[:].rearrange("p (o e) -> p o e", o=1).to_broadcast([P, G4, E]),
                          ALU.add).then_inc(M.gate_read, 1)
        dve.wait_ge(M.gate_read, g + 1)
        choose(dve, M, T, T.logits[:, :, :], T.best[:, :], T.pick1[:, :, :], at)
        dve.scalar_tensor_tensor(T.others[:, :, :], T.pick1[:, :, :], -1e38, T.logits[:, :, :],
                                 ALU.mult, ALU.add).then_inc(M.route, 1)
        dve.wait_ge(M.route, at + 6)
        choose(dve, M, T, T.others[:, :, :], T.best2[:, :], T.pick2[:, :, :], at + 6)
        dve.tensor_tensor(T.diff[:, :], T.best2[:, :], T.best[:, :], ALU.subtract).then_inc(M.route, 1)
        dve.wait_ge(M.exp_done, g + 1)
        dve.tensor_scalar(T.den[:, :], T.e2[:, :], 1.0, None, ALU.add).then_inc(M.route, 1)
        dve.wait_ge(M.route, at + 13)
        dve.reciprocal(T.g1[:, :], T.den[:, :]).then_inc(M.route, 1)
        dve.wait_ge(M.route, at + 14)
        dve.tensor_tensor(T.g2[:, :], T.e2[:, :], T.g1[:, :], ALU.mult).then_inc(M.route, 1)
        dve.wait_ge(M.route, at + 15)
        dve.tensor_tensor(T.pick1[:, :, :], T.pick1[:, :, :], spread(T.g1[:, :], E), ALU.mult).then_inc(M.route, 1)
        dve.tensor_tensor(T.pick2[:, :, :], T.pick2[:, :, :], spread(T.g2[:, :], E), ALU.mult).then_inc(M.route, 1)
        dve.wait_ge(M.route, at + 17)
        dve.tensor_tensor(T.gates[:, :, :], T.pick1[:, :, :], T.pick2[:, :, :], ALU.add).then_inc(M.route, 1)

        def add(k, a, what):
            n = G4 * ((E + 1) * g + k) + a
            if k:
                dve.wait_ge(M.acc, n - G4 + 1)
            what().then_inc(M.acc, 1)

        dve.wait_ge(M.b2_done, g + 1)
        wait(dve, M.x_out, G4 * g)
        for a in range(G4):
            add(0, a, lambda: dve.tensor_tensor(T.sum[:, a, :], T.mi[1][:, a * P:(a + 1) * P], T.xf[p][:, a, :],
                                                ALU.add))
        for e in range(E):
            dve.wait_ge(M.y_done, E * HC * g + HC * (e + 1))
            for a in range(G4):
                add(e + 1, a, lambda: dve.scalar_tensor_tensor(
                    T.sum[:, a, :], T.yb[e % 2][:, a * P:(a + 1) * P], T.gates[:, a, e:e + 1], T.sum[:, a, :],
                    ALU.mult, ALU.add))
        layernorm_group(dve, M, T, g, x_to)

    groups(dve, body)

def tiled(a, width):
    return np.ascontiguousarray(a.reshape(2, P, width).transpose(1, 0, 2)).astype(np.float32)


def constants():
    causal = np.where(np.arange(P)[None, :] > np.arange(P)[:, None], BIG, 0.0)
    r, c = np.arange(P)[:, None], np.arange(WIN)[None, :]
    band = [np.where(np.abs(r + off - c) <= HALF, 0.0, BIG) for off in (0, P - (S - WIN))]
    inv = (1.0 / np.float32(10000.0) ** (np.arange(0, DH, 2, dtype=np.float32) / np.float32(DH))).astype(np.float32)
    ang = np.arange(S, dtype=np.float32)[:, None] * inv[None, :]
    ninth = np.zeros((4, 32, 4, 4, 2, 16), np.float32)
    for t in range(4):
        for j in range(4):
            ninth[t, 0:NG, j, t, j % 2, DH] = 1.0 / W_GLOBAL
    return {
        "ident": np.eye(P),
        "causal": np.tile(causal, (1, 4)),
        "band": np.concatenate([np.tile(m, (1, 4)) for m in band], axis=1),
        "cos": tiled(np.concatenate([np.cos(ang)] * 2, axis=1), DH),
        "sin": tiled(np.concatenate([-np.sin(ang), np.sin(ang)], axis=1), DH),
        "ninth": ninth.reshape(P, 4 * P),
        "diag": np.repeat(np.eye(4), 32, axis=0).repeat(DH, axis=1),
        "kidx": np.arange(2)[None, :] * P + np.arange(P)[:, None],
        "first": np.tile(np.arange(8, 0, -1), (P, 4)),
    }


class Tensors:
    pass


def build(nc, a):
    with ExitStack() as ctx:
        def sb(name, shape, dt=F32):
            return ctx.enter_context(nc.sbuf_tensor(name, shape, dt))

        def sem(name):
            return ctx.enter_context(nc.semaphore(name))

        bank = [ctx.enter_context(nc.psum_tensor(f"bank{i}", [P, 512], F32)) for i in range(8)]
        T = Tensors()
        T.ident, T.identb = sb("ident", [P, P]), sb("identb", [P, P], BF16)
        T.causal, T.band = sb("causal", [P, 512], BF16), sb("band", [P, 8 * WIN], BF16)
        T.cos, T.sin = sb("cos", [P, 2, DH]), sb("sin", [P, 2, DH])
        T.xin, T.xt = sb("xin", [P, 2, 2, D]), sb("xt", [P, S])
        T.rq, T.rs = sb("rq", [P, 2, 2 * D]), sb("rs", [P, 2, 2 * D])
        T.tsr = sb("ts", [P, 2, 8 * P], F32R)
        T.ts = T.tsr[:, :, :].bitcast(F32)
        T.vtmp = sb("vtmp", [P, 2, D])
        T.vb = [sb(f"vb{i}", [P, 2, 4, 4, 32]) for i in range(2)]
        T.qs = [sb(f"qs{i}", [P, 4, S], F32R) for i in range(2)]
        T.ks = [sb(f"ks{i}", [P, 4, S], F32R) for i in range(2)]
        T.p = [sb(f"p{i}", [P, 4, 512]) for i in range(2)]
        T.nm, T.dm = sb("nm", [P, 2, 2, 8]), sb("dm", [P, 8])
        T.mspr = sb("msp", [P, 2, 2, 16], F32R)
        T.msp = T.mspr[:, :, :, :].bitcast(F32)
        T.mt = [sb(f"mt{j}", [16, S], F32R) for j in range(4)]
        T.ovs, T.ogs = sb("ovs", [P, 2, S]), sb("ogs", [P, 2, S])
        T.rd = sb("rd", [P, 2, 32])
        T.on, T.ong, T.ot = sb("on", [P, 2, D]), sb("ong", [P, 2 * D]), sb("ot", [P, S])
        T.r, T.st, T.mv, T.rs2 = sb("r", [P, 2, D]), sb("st", [P, 2, 6]), sb("mv", [P, 2, 2]), sb("rs2", [P, 2])
        T.ve, T.mhalf = sb("ve", [P, 2]), sb("mhalf", [P, 4])
        T.kg = [sb(f"kg{i}", [P, 4, 32], F32R) for i in range(2)]
        T.pick, T.pick4 = sb("pick", [P, 2, NGE], F32R), sb("pick4", [P, 2, 4, 32])
        T.vgb = [sb(f"vgb{i}", [P, 4, P]) for i in range(2)]
        T.diag = sb("diag", [P, 4 * DH])
        kidx, gi, gif = sb("kidx", [P, 2]), sb("gi", [P, NG], mybir.dt.int32), sb("gif", [P, NG])
        x_a, x_b = sb("x_a", [P, NT, D]), sb("x_b", [P, NT, D])
        stage = x_b[:, 0:16, :].rearrange("p a d -> p (a d)")

        T.xf, T.xt4 = [sb(f"xf{i}", [P, G4, D]) for i in range(2)], [sb(f"xt4_{i}", [P, G4 * P]) for i in range(2)]
        T.sum, T.st4, T.mv4 = sb("sum", [P, G4, D]), sb("st4", [P, G4, 6]), sb("mv4", [P, G4, 2])
        T.ve4, T.rs4, T.first = sb("ve4", [P, G4]), sb("rs4", [P, G4]), sb("first", [P, G4 * E])
        T.eq, T.rank, T.gates, T.logits, T.others, T.pick1, T.pick2 = (
            sb(n, [P, G4, E]) for n in ("eq", "rank", "gates", "logits", "others", "pick1", "pick2"))
        T.best, T.best2, T.top, T.diff, T.e2, T.den, T.g1, T.g2 = (
            sb(n, [P, G4]) for n in ("best", "best2", "top", "diff", "e2", "den", "g1", "g2"))
        T.gt, T.h = sb("gt", [E, G4 * P]), [sb(f"h{i}", [P, G4 * P]) for i in range(4)]
        T.y2, T.hb, T.yb = [bank[2:4], bank[4:6]], bank[2:4], bank[4:6]
        F0, F1 = Mixture("f0", 5, E + 1, sem), Mixture("f1", 18, E + 1, sem)
        V0, V1 = Tensors(), Tensors()
        V0.gate, V0.expert = sb("gate", [P, E]), sb("expert", [P, E * D])
        V1.router, V1.rb, V1.b1, V1.b2 = sb("router", [P, E]), sb("rb", [P, E]), sb("b1", [P, E * HC]), sb("b2", [E, D])
        V1.w1, V1.w2 = sb("w1", [P, E, HID]), sb("w2", [P, E, HC, D])
        T.mi, T.s1, T.ov = [bank[0], bank[1]], [bank[2], bank[3]], bank[4]
        L0, L1 = Attention("l0", False, sem), Attention("l1", True, sem)
        T.s2, T.og = [bank[5], bank[6], bank[7]], bank[7]
        x_dram = a["x"]
        W0, W1 = Tensors(), Tensors()
        W0.qkv, W0.out = sb("w0_qkv", [P, 3 * D]), sb("w0_out", [P, D])
        W0.x_batch = lambda b: x_dram[bass.ds(b, 1), :, :].rearrange("o (a p) d -> p (o a) d", p=P)
        W0.resid, W0.x_next = x_a, x_b
        W1.qkv, W1.out = sb("w1_qkv", [P, 3 * D]), sb("w1_out", [P, D])
        W1.bqkv, bo = sb("b1_qkv", [P, 3 * D]), sb("bo", [P, D])

        const_in, stage_in, x_a_in, stored = sem("const_in"), sem("stage_in"), sem("x_a_in"), sem("stored")
        ready, zeroed, preset = sem("ready"), sem("zeroed"), sem("preset")
        gi_f, vg_in, bo_added, again = sem("gi_f"), sem("vg_in"), sem("bo_added"), sem("again")
        loads = [(T.ident, "ident"), (W0.qkv, "w0_qkv"), (T.cos, "cos"), (T.sin, "sin"), (W0.out, "w0_out"),
                 (T.diag, "diag"), (T.first, "first"), (V0.gate, "gate"), (V0.expert, "expert"), (V1.router, "router"),
                 (V1.b1, "b1"), (V1.b2, "b2"), (V1.w1, "w1"), (V1.w2, "w2"), (kidx, "kidx"), (W1.qkv, "w1_qkv"), (W1.out, "w1_out")]
        rows = [(gi, "gi"), (W1.bqkv, "b1_qkv"), (bo, "bo"), (V1.rb, "rb")]
        n_const = 16 * (len(loads) + len(rows))
        x_c = sb("x_c", [P, NT, D])
        W1.x_batch = lambda b: x_a[:, bass.ds(2 * b, 2), :]
        W1.resid, W1.x_next = x_c, x_b
        block = ctx.enter_context(nc.Block())

        @block.sync
        def _(sp):
            for t, name in loads:
                sp.dma_start(t.ap(), a[name]).then_inc(const_in, 16)
            for t, name in rows:
                sp.dma_start(t.ap(), a[name].to_broadcast([P, a[name].shape[1]])).then_inc(const_in, 16)
            sp.dma_start(stage[:, 0:512], a["causal"]).then_inc(stage_in, 16)
            sp.dma_start(stage[:, 512:512 + 8 * WIN], a["band"]).then_inc(stage_in, 16)
            sp.dma_start(x_a[:, :, :], x_dram.rearrange("b (a p) d -> p (b a) d", p=P)).then_inc(x_a_in, 16)
            for g in T.vgb:
                sp.dma_start(g.ap(), a["ninth"].rearrange("p (j c) -> p j c", j=4)).then_inc(vg_in, 16)
            attention_sp(sp, L0, T, W0)
            sp.wait_ge(L0.x_out, NT)
            mixture_sp(sp, F0, T, x_b)
            sp.wait_ge(F0.x_out, NT)
            attention_sp(sp, L1, T, W1)
            sp.wait_ge(L1.x_out, NT)
            mixture_sp(sp, F1, T, x_b)
            out = a["out"].rearrange("b (a p) d -> p (b a) d", p=P)
            for g in range(GROUPS):
                sp.wait_ge(F1.x_out, G4 * (g + 1))
                sp.dma_start(out[:, G4 * g:G4 * (g + 1), :], x_a[:, G4 * g:G4 * (g + 1), :]).then_inc(stored, 16)
            sp.wait_ge(stored, 16 * GROUPS)

        @block.tensor
        def _(pe):
            pe.wait_ge(const_in, n_const)
            pe.wait_ge(ready, 5)
            pe.wait_ge(preset, 4)
            attention_pe(pe, L0, T, W0)
            one_expert_pe(pe, F0, T, V0)
            pe.wait_ge(vg_in, 32)
            pe.wait_ge(preset, 6)
            pe.wait_ge(F0.gate_read, GROUPS)
            pe.wait_ge(F0.acc, F0.per_tile * NT)
            attention_pe(pe, L1, T, W1)
            pe.wait_ge(L1.exp_done, 4 * 4 * B)
            pe.wait_ge(L1.r_done, B)
            pe.wait_ge(L1.red_done, 4 * 4 * B)
            two_experts_pe(pe, F1, T, V1)

        @block.scalar
        def _(act):
            act.wait_ge(preset, 4)
            attention_act(act, L0, T, W0)
            one_expert_act(act, F0, T)
            attention_act(act, L1, T, W1)
            two_experts_act(act, F1, T, V1)

        @block.vector
        def _(dve):
            dve.wait_ge(const_in, n_const)
            dve.wait_ge(stage_in, 32)
            dve.tensor_copy(T.identb[:], T.ident[:]).then_inc(ready, 1)
            dve.tensor_copy(T.causal[:], stage[:, 0:512]).then_inc(ready, 1)
            dve.tensor_copy(T.band[:], stage[:, 512:512 + 8 * WIN]).then_inc(ready, 1)
            dve.tensor_copy(gif[:], gi[:]).then_inc(gi_f, 1)
            dve.wait_ge(gi_f, 1)
            dve.wait_ge(zeroed, 7)
            for kt in range(2):
                dve.tensor_scalar(T.pick[:, kt, 0:NG], gif[:], kidx[:, kt:kt + 1], None,
                                  ALU.is_equal).then_inc(ready, 1)
            for kt in range(2):
                dve.tensor_scalar(T.pick4[:, kt, :, 0:NG], gif[:].rearrange("p (o g) -> p o g", o=1).to_broadcast([P, 4, NG]),
                                  kidx[:, kt:kt + 1], None, ALU.is_equal).then_inc(ready, 1)
            dve.wait_ge(x_a_in, 16)
            attention_dve(dve, L0, T, W0)
            one_expert_dve(dve, F0, T, x_a)
            dve.wait_ge(bo_added, 1)
            dve.wait_ge(vg_in, 32)
            attention_dve(dve, L1, T, W1)
            two_experts_dve(dve, F1, T, V1, x_a)

        @block.gpsimd
        def _(pool):
            pool.memset(T.mhalf[:], -0.5).then_inc(zeroed, 1)
            pool.memset(T.pick[:, :, :].bitcast(F32), 0.0).then_inc(zeroed, 1)
            pool.memset(T.pick4[:, :, :, :], 0.0).then_inc(zeroed, 1)
            pool.memset(T.ts[:, :, :], 0.0).then_inc(zeroed, 1)
            for par in range(2):
                pool.memset(T.vb[par][:, :, :, :, :], 0.0).then_inc(zeroed, 1)
            for par in range(2):
                m = pool.memset(T.kg[par][:, :, :].bitcast(F32), 0.0)
            m.then_inc(zeroed, 1)
            pool.wait_ge(zeroed, 7)
            keys = T.ts[:, :, :].rearrange("p a (h c) -> p a h c", c=32)[:, :, 16:32, 24:28]
            pool.memset(keys, 1.0).then_inc(preset, 1)
            pool.memset(T.mspr[:, :, :, :].bitcast(F32), 0.0).then_inc(preset, 1)

            def ninth_column(value, signal):
                for par in range(2):
                    for s in range(2):
                        m = pool.memset(T.vb[par][:, :, s::2, :, 16 * s + DH], value)
                    m.then_inc(signal, 1)

            ninth_column(1.0, preset)
            attention_pool(pool, L0, T, W0)
            mixture_pool(pool, F0, T)
            pool.wait_ge(L0.pv_done, 4 * B)
            ninth_column(1.0 / W_LOCAL, preset)
            pool.wait_ge(F0.x_out, NT)
            pool.tensor_tensor(x_c[:, :, :], x_a[:, :, :],
                               bo[:].rearrange("p (o d) -> p o d", o=1).to_broadcast([P, NT, D]),
                               ALU.add).then_inc(bo_added, 1)
            attention_pool(pool, L1, T, W1)
            mixture_pool(pool, F1, T)


def out_rows(w):
    return np.ascontiguousarray(w.reshape(4, 2, 2, DH, D).transpose(1, 0, 2, 3, 4).reshape(D, D))


def kernel(L0_attn_x, L0_attn_w_qkv, L0_attn_w_out, L0_ffn_gate_w, L0_ffn_expert_w, L1_attn_Wq, L1_attn_bq,
           L1_attn_Wk, L1_attn_bk, L1_attn_Wv, L1_attn_bv, L1_attn_Wo, L1_attn_bo, L1_attn_global_indices,
           L1_ffn_router_w, L1_ffn_router_b, L1_ffn_w1, L1_ffn_b1, L1_ffn_w2, L1_ffn_b2):
    import concourse.bacc as bacc
    from concourse.bass_utils import run_bass_kernel_spmd

    def turned(w):
        return np.asarray(w).T

    arrays = {k: v.astype(np.float32) for k, v in constants().items()}
    arrays.update(
        x=L0_attn_x, w0_qkv=L0_attn_w_qkv, w0_out=out_rows(np.asarray(L0_attn_w_out)),
        gate=turned(L0_ffn_gate_w),
        expert=np.asarray(L0_ffn_expert_w).transpose(2, 0, 1).reshape(D, E * D),
        w1_qkv=np.concatenate([turned(L1_attn_Wq), turned(L1_attn_Wk), turned(L1_attn_Wv)], axis=1),
        b1_qkv=np.concatenate([L1_attn_bq, L1_attn_bk, L1_attn_bv])[None, :],
        w1_out=out_rows(turned(L1_attn_Wo)), bo=np.asarray(L1_attn_bo)[None, :],
        gi=np.asarray(L1_attn_global_indices)[None, :],
        router=L1_ffn_router_w, rb=np.asarray(L1_ffn_router_b)[None, :],
        w1=np.asarray(L1_ffn_w1).transpose(1, 0, 2),
        b1=np.asarray(L1_ffn_b1).reshape(E * HC, P).T,
        w2=np.asarray(L1_ffn_w2).reshape(E, HC, P, D).transpose(2, 0, 1, 3), b2=L1_ffn_b2)
    arrays = {k: np.ascontiguousarray(v) for k, v in arrays.items()}

    nc = bacc.Bacc("TRN2", target_bir_lowering=False, num_devices=1)
    a = {k: nc.dram_tensor(f"in_{k}", v.shape, mybir.dt.from_np(v.dtype), kind="ExternalInput").ap()
         for k, v in arrays.items()}
    a["out"] = nc.dram_tensor("result", (B, S, D), F32, kind="ExternalOutput").ap()
    build(nc, a)
    r = run_bass_kernel_spmd(nc, [{f"in_{k}": v for k, v in arrays.items()}], core_ids=[0])
    return r.results[0]["result"]
```

```python
from contextlib import ExitStack

import numpy as np

import concourse.bass as bass
from concourse import mybir

F32 = mybir.dt.float32
F32R = mybir.dt.float32r
ALU = mybir.AluOpType
ACT = mybir.ActivationFunctionType
AX = mybir.AxisListType

P = 128
D = 128
S = 256
B = 16
NT = B * S // P
DH = 8
SCALE = float(DH) ** -0.5
EPS = 1e-5
HALF = 32
WIN = P + HALF
NG = 25
NGE = 26
WG = NGE + WIN
KW = 2 * NGE + S
BIG = -1e30
W_LOCAL, W_GLOBAL = 0.7, 0.3


class Attention:

    def __init__(self, name, local, sem, passed):
        self.local = local
        self.units = 4 if local else 3
        self.ring1 = 2 if local else 3
        self.ring2 = 2
        self.parts = 4 if local else 2
        self.kept = 2 if local else 1

        def s(what):
            return sem(f"{name}_{what}")

        self.x_in = [s("x_in0"), s("x_in1")]
        self.xt_done, self.xt_kept = s("xt_done"), s("xt_kept")
        self.pj_done, self.pj_kept = s("pj_done"), s("pj_kept")
        self.sum_done = s("sum_done")
        self.hi_done, self.ts_done = s("hi_done"), s("ts_done")
        self.sk_done = s("sk_done")
        self.q_kept, self.k_kept = s("q_kept"), s("k_kept")
        self.q_in = [s(f"q_in{j}") for j in range(4)]
        self.p1_done, self.red_done = s("p1_done"), s("red_done")
        self.msp_hi, self.msp_done = s("msp_hi"), s("msp_done")
        self.mx_done, self.mx_kept = s("mx_done"), s("mx_kept")
        self.mrow = [s(f"mrow{j}") for j in range(4)]
        self.p2_done, self.exp_done = s("p2_done"), s("exp_done")
        self.passed = passed
        self.masked = s("masked")
        self.vpad = s("vpad")
        self.pv_done, self.ov_kept = s("pv_done"), s("ov_kept")
        self.ot_done, self.rden, self.on_half, self.on_done = s("ot_done"), s("rden"), s("on_half"), s("on_done")
        self.ont_done, self.ot_kept = s("ont_done"), s("ot_kept")
        self.y_done, self.r_done = s("y_done"), s("r_done")
        self.stats, self.aggr = s("stats"), s("aggr")
        self.var_eps, self.rstd, self.x_out = s("var_eps"), s("rstd"), s("x_out")
        if local:
            self.vg_done, self.vg_kept = s("vg_done"), s("vg_kept")
            self.kg_done, self.kg_kept = s("kg_done"), s("kg_kept")
            self.xb_done = s("xb_done")


class There:

    def __init__(self, i, inner):
        self.turn_x = inner or -1 <= i <= B - 3
        self.prep = inner or -1 <= i <= B - 2
        self.scores = inner or 0 <= i < B
        self.late = inner or 1 <= i <= B
        self.finish = inner or 2 <= i <= B + 1
        self.pass2 = [self.late if j < 3 else self.scores for j in range(4)]
        self.inner = inner
        self.first = not inner and i == -1

    def max_step(self, j):
        return self.late if j == 0 else self.scores


def iterations(eng, body):
    for i in (-1, 0, 1):
        body(i, i % 2, There(i, False))
    with eng.Fori(2, B - 3, 2) as i:
        body(i, 0, There(i, True))
        body(i + 1, 1, There(i, True))
    for i in range(B - 2, B + 2):
        body(i, i % 2, There(i, False))


def wait(eng, sem, value):
    if not isinstance(value, int) or value > 0:
        eng.wait_ge(sem, value)


def wait_apart(eng, passed, sem, value):
    if not isinstance(value, int) or value > 0:
        eng.wait_ge(sem, value).then_inc(passed, 1)


def local_items(u):
    return range(3 * u, min(3 * u + 3, 8))


ROUNDS = (("pj0", "og", "mx0", "ont", "mx1", "y", "q1", "xt", "mx3"),
          ("ot", "pj1", "q0", "vg", "mx2", "k0", "k1", "kg"))


MX_BANK = (0, 0, 1, 0)


def attention_pe(pe, L, T, W):

    def turn(out, in_):
        return pe.transpose(out, in_, T.ident[:])

    def turn_exact(out, in_):
        return pe.transpose(out.bitcast(F32R), in_, T.identr[:])

    def in_iteration(name, i, th):
        if name in ("og", "vg", "kg") and not L.local:
            return False
        if name in ("ot", "og", "ont", "y"):
            return th.finish
        if name[:2] == "mx":
            return th.max_step(int(name[2]))
        return th.scores if name == "vg" else th.turn_x if name == "xt" else th.prep

    def bank_read(name, i, th):
        bank = ROUNDS[name in ROUNDS[1]]
        before = [(x, i, th) for x in bank[:bank.index(name)]]
        if th.inner:
            before = [(x, i - 1, th) for x in bank] + before
        else:
            before = [(x, k, There(k, False)) for k in range(-1, i) for x in bank] + before
        before = [x for x in before if in_iteration(*x)]
        if not before:
            return
        last, k, _ = before[-1]
        signal, value = {
            "ot": (L.on_done, k - 1), "og": (L.on_done, k - 1), "ont": (L.ot_kept, k - 1), "y": (L.r_done, k - 1),
            "mx0": (L.mx_kept, 4 * k), "mx1": (L.mx_kept, 4 * k + 1), "mx2": (L.mx_kept, 4 * k + 2),
            "mx3": (L.mx_kept, 4 * k + 3), "pj0": (L.pj_kept, 2 * k + 3), "pj1": (L.pj_kept, 2 * k + 4),
            "q0": (L.q_kept, 2 * k + 3), "q1": (L.q_kept, 2 * k + 4), "k0": (L.k_kept, 2 * k + 3),
            "k1": (L.k_kept, 2 * k + 4), "xt": (L.xt_kept, k + 3),
            "vg": (L.vg_kept if L.local else None, k + 1), "kg": (L.kg_kept if L.local else None, k + 2)}[last]
        wait(pe, signal, value)

    def body(i, p, th):
        n = 1 - p
        fin = i - 2

        def round_ot():
            bank_read("ot", i, th)
            pe.wait_ge(L.ov_kept, L.kept * fin + 1)
            for tau in range(2):
                for r in range(2):
                    m = turn(T.mi[1][:, (2 * tau + r) * P:(2 * tau + r + 1) * P],
                             T.ovs[:, r, tau * P:(tau + 1) * P])
            m.then_inc(L.ot_done, 1)

        def round_og():
            bank_read("og", i, th)
            pe.wait_ge(L.ov_kept, L.kept * fin + 2)
            for tau in range(2):
                for r in range(2):
                    m = turn(T.mi[0][:, (2 * tau + r) * P:(2 * tau + r + 1) * P],
                             T.ogs[:, r, tau * P:(tau + 1) * P])
            m.then_inc(L.ot_done, 1)

        def round_xt(batch, par):
            if not (isinstance(batch, int) and batch == 0):
                bank_read("xt", i, th)
            pe.wait_ge(L.x_in[par], 8 * (batch - par) + 16)
            for tau in range(2):
                m = turn(T.mi[0][:, tau * P:(tau + 1) * P], T.xin[:, par, tau, :])
            m.then_inc(L.xt_done, 1)

        def round_vg():
            bank_read("vg", i, th)
            pe.wait_ge(L.pj_kept, 2 * i + 2)
            for kt in range(2):
                m = pe.matmul(T.mi[1][:, 0:P], T.pick4[:, kt, :], T.vtmp[:, p, kt, :], start=kt == 0, stop=kt == 1)
            m.then_inc(L.vg_done, 1)

        def round_pj(tau):
            bank_read(f"pj{tau}", i, th)
            pe.wait_ge(L.xt_kept, i + 2)
            m = pe.matmul(T.mi[tau][:, 0:3 * D], T.xt[:, tau * P:(tau + 1) * P], W.qkv[:], start=True, stop=True)
            m.then_inc(L.pj_done, 1)

        def round_ont():
            bank_read("ont", i, th)
            pe.wait_ge(L.on_done, fin + 1)
            for tau in range(2):
                m = turn(T.mi[0][:, tau * P:(tau + 1) * P], T.on[:, tau, :])
            m.then_inc(L.ont_done, 1)

        def round_y():
            bank_read("y", i, th)
            pe.wait_ge(L.ot_kept, fin + 1)
            for tau in range(2):
                m = pe.matmul(T.mi[0][:, tau * P:(tau + 1) * P], T.ot[:, tau * P:(tau + 1) * P], W.out[:],
                              start=tau == 0, stop=True, skip_group_check=True)
            m.then_inc(L.y_done, 1)

        def round_mx(j):
            bank_read(f"mx{j}", i, th)
            pe.wait_ge(L.msp_done, 4 * i + j)
            rows = 4 * L.parts
            for tau in range(2):
                m = turn_exact(T.mi[MX_BANK[j]][0:rows, tau * P:(tau + 1) * P],
                               T.mspr[:, (j + 1) % 2, tau, 0:rows])
            m.then_inc(L.mx_done, 1)

        def round_stack(keys, tau):
            name = f"{'qk'[keys]}{tau}"
            bank_read(name, i, th)
            pe.wait_ge(L.ts_done, 2 * (i + 1) + tau + 1)
            bank = T.mi[name in ROUNDS[1]]
            for t in range(4):
                m = turn_exact(bank[:, t * P:(t + 1) * P],
                               T.tsr[:, tau, (4 * keys + t) * P:(4 * keys + t + 1) * P])
            m.then_inc(L.sk_done, 1)

        def round_kg():
            bank_read("kg", i, th)
            pe.wait_ge(L.ts_done, 2 * (i + 1) + 2)
            for t in range(4):
                for kt in range(2):
                    m = pe.matmul(T.mi[1][:, t * 32:t * 32 + NGE], T.tsr[:, kt, (4 + t) * P:(5 + t) * P],
                                  T.pick[:, kt, :], start=t == 0 and kt == 0, stop=kt == 1, skip_group_check=True)
            m.then_inc(L.kg_done, 1)

        def pass1(j, u):
            unit = L.units * (4 * i + j) + u
            bank = T.s1[u % L.ring1]
            if u == 0 and j == 0:
                pe.wait_ge(L.k_kept, 2 * i + 2)
                if L.local:
                    pe.wait_ge(L.kg_kept, i + 1)
            if u == 0:
                pe.wait_ge(L.q_in[j], 16 * i + 16)
            wait(pe, L.red_done, unit - L.ring1 + 1)
            q, k = T.qs[p][j], T.ks[p]
            if L.local:
                for c in range(2):
                    tau, t = divmod(2 * u + c, 4)
                    lo = tau * (KW - WG)
                    m = pe.matmul(bank[:, c * WG:(c + 1) * WG], q[:, t, tau * P:(tau + 1) * P],
                                  k[:, t, lo:lo + WG], start=c == 0, stop=True, skip_group_check=True)
            elif u == 0:
                for t in range(4):
                    m = pe.matmul(bank[:, t * P:(t + 1) * P], q[:, t, 0:P], k[:, t, NGE:NGE + P],
                                  start=t == 0, stop=True, skip_group_check=True)
            else:
                for c in range(2):
                    t = 2 * (u - 1) + c
                    m = pe.matmul(bank[:, c * S:(c + 1) * S], q[:, t, P:S], k[:, t, NGE:NGE + S],
                                  start=c == 0, stop=True, skip_group_check=True)
            m.then_inc(L.p1_done, 1)

        def pass2(j, u):
            js = (j + 1) % 4
            par, batch = (n, i - 1) if j < 3 else (p, i)
            unit = L.units * (4 * i + j - 3) + u
            bank = T.s2[u % 2 if L.local else (j + u) % 2]
            if u == 0:
                pe.wait_ge(L.mrow[js], 16 * batch + 16)
            wait_apart(pe, L.passed, L.exp_done, unit - L.ring2 + 1)
            q, k = T.qs[par][js], T.ks[par]
            if L.local and u == 3:
                for t in range(4):
                    m = pe.matmul(bank[32 * t:32 * t + 32, 0:S], T.kg[par][:, t, :], q[:, t, :].bitcast(F32),
                                  start=True, stop=True)
            elif L.local:
                for c, item in enumerate(local_items(u)):
                    kt, t = divmod(item, 4)
                    lo = kt * (S - WIN)
                    m = pe.matmul(bank[:, c * WIN:(c + 1) * WIN], k[:, t, NGE + kt * P:NGE + (kt + 1) * P],
                                  q[:, t, lo:lo + WIN], start=c == 0, stop=True, skip_group_check=True)
            elif u == 0:
                for t in range(4):
                    m = pe.matmul(bank[:, t * P:(t + 1) * P], k[:, t, NGE + P:NGE + S], q[:, t, P:S],
                                  start=t == 0, stop=True, skip_group_check=True)
            else:
                for c in range(2):
                    t = 2 * (u - 1) + c
                    m = pe.matmul(bank[:, c * S:(c + 1) * S], k[:, t, NGE:NGE + P], q[:, t, :],
                                  start=c == 0, stop=True, skip_group_check=True)
            m.then_inc(L.p2_done, 1)

        def pv(j, part):
            step = 4 * (i - 1) + j
            pb = T.p[j % 2]
            r = j // 2
            if j == 0 and part == 0:
                pe.wait_ge(L.vpad, i)
                wait(pe, L.ov_kept, L.kept * (i - 1))
            if part == 2:
                if j == 0:
                    pe.wait_ge(L.vg_kept, i)
                pe.wait_ge(L.exp_done, 4 * step + 4)
                m = pe.matmul(T.og[:, r * S:(r + 1) * S], T.vgb[n][:, j, :], pb[:, 3, 0:S],
                              start=j == 0, stop=False, skip_group_check=True)
            elif L.local:
                pe.wait_ge(L.masked, 4 * step + 3 + part)
                flat = pb[:, :, :].rearrange("p u c -> p (u c)")
                for t in range(4):
                    item = 4 * part + t
                    lo = r * S + part * (S - WIN)
                    m = pe.matmul(T.ov[32 * t:32 * t + 32, lo:lo + WIN], T.vb[n][:, part, j, t, :],
                                  flat[:, item * WIN:(item + 1) * WIN],
                                  start=j == 0 and part == 0, stop=False, skip_group_check=True)
            else:
                pe.wait_ge(L.masked, 3 * step + 3)
                for t in range(4):
                    if part == 0:
                        m = pe.matmul(T.ov[32 * t:32 * t + 32, r * S:(r + 1) * S], T.vb[n][:, 0, j, t, :],
                                      pb[:, 1 + t // 2, t % 2 * S:(t % 2 + 1) * S],
                                      start=j == 0, stop=False, skip_group_check=True)
                    else:
                        m = pe.matmul(T.ov[32 * t:32 * t + 32, r * S + P:(r + 1) * S], T.vb[n][:, 1, j, t, :],
                                      pb[:, 0, t * P:(t + 1) * P],
                                      start=False, stop=False, skip_group_check=True)
            if part == L.kept:
                m.then_inc(L.pv_done, 1)

        if th.first:
            round_xt(0, 0)
        for j in range(4):
            for u in range(L.units):
                if th.scores:
                    pass1(j, u)
                if j in (0, 1) and u == 0 and th.prep:
                    round_pj(j)
                if j == 0 and u == 1 and th.finish:
                    round_ot()
                if j == 0 and u == 2 and th.finish and L.local:
                    round_og()
                if j == 1 and u == (1 if L.local else 0) and th.finish:
                    round_ont()
                if j == 2 and u == 1 and L.local and th.scores:
                    round_vg()
                if j == 2 and u == 0 and th.finish:
                    round_y()
                if j == 3 and u in (0, 2) and th.prep:
                    round_stack(1, u // 2)
                if j == 3 and u == 0 and th.turn_x:
                    round_xt(i + 2, p)
                if u == L.units - 1 and th.max_step(j) and not (L.local and j == 0):
                    round_mx(j)
                if th.pass2[j]:
                    pass2(j, u)
                if th.late and u > 0:
                    pv(j, u - 1)
            if j in (1, 2) and th.prep:
                round_stack(0, j - 1)
            if L.local and j == 0 and th.max_step(j):
                round_mx(j)
        if L.local and th.prep:
            round_kg()

    iterations(pe, body)


def attention_act(act, L, T, W):

    def body(i, p, th):
        n = 1 - p
        fin = i - 2

        def keep_pv():
            act.wait_ge(L.pv_done, 4 * fin + 4)
            if not (isinstance(i, int) and i == 2):
                act.wait_ge(L.ot_done, L.kept * fin)
            act.copy(T.ovs[:, :, :], T.ov[:, :].rearrange("p (r q) -> p r q", r=2)).then_inc(L.ov_kept, 1)
            if L.local:
                act.copy(T.ogs[:, :, :], T.og[:, :].rearrange("p (r q) -> p r q", r=2)).then_inc(L.ov_kept, 1)

        def keep_xt(batch):
            act.wait_ge(L.xt_done, batch + 1)
            wait(act, L.pj_done, 2 * batch)
            act.copy(T.xt[:, :], T.mi[0][:, 0:S]).then_inc(L.xt_kept, 1)

        def keep_mx(j):
            js = (j + 3) % 4
            batch = i - 1 if j == 0 else i
            act.wait_ge(L.mx_done, 4 * i + j)
            wait(act, L.mrow[js], 16 * batch)
            rows = 4 * L.parts
            act.copy(T.mt[js][0:rows, :], T.mi[MX_BANK[j]][0:rows, 0:S]).then_inc(L.mx_kept, 1)

        def split_hi(tau):
            act.wait_ge(L.sum_done, 2 * (i + 1) + tau + 1)
            wait(act, L.sk_done, 4 * (i + 1))
            if L.local:
                wait(act, L.kg_done, i + 1)
            ts = T.tsr[:, tau, :].rearrange("p (h c d) -> p h c d", h=32, d=DH)
            rq = T.rq[:, tau, :].rearrange("p (h o d) -> p h o d", h=32, o=1)
            act.copy(ts[:, 0:16, 0:3:2, :], rq[:, 0:16].to_broadcast([P, 16, 2, DH]))
            act.copy(ts[:, 16:32, 0:2, :], rq[:, 16:32].to_broadcast([P, 16, 2, DH])).then_inc(L.hi_done, 1)

        def keep_ot():
            act.wait_ge(L.ont_done, fin + 1)
            wait(act, L.y_done, fin)
            act.copy(T.ot[:, :], T.mi[0][:, 0:S]).then_inc(L.ot_kept, 1)

        def keep_stack(keys, tau):
            act.wait_ge(L.sk_done, 4 * (i + 1) + 2 * keys + tau + 1)
            from_ = T.mi[f"{'qk'[keys]}{tau}" in ROUNDS[1]][:, :].rearrange("p (t q) -> p t q", t=4)
            if keys:
                act.copy(T.ks[n][:, :, NGE + tau * P:NGE + (tau + 1) * P], from_).then_inc(L.k_kept, 1)
            else:
                for q_in in L.q_in:
                    wait(act, q_in, 16 * (i + 1))
                act.copy(T.qf[:, :, tau * P:(tau + 1) * P], from_).then_inc(L.q_kept, 1)

        def exp(j, u):
            step = 4 * i + j - 3
            pb = T.p[(j + 1) % 2]
            bank = T.s2[u % 2 if L.local else (j + u) % 2]
            cols = (S if u == 3 else len(local_items(u)) * WIN) if L.local else 512
            act.wait_ge(L.p2_done, L.units * step + u + 1)
            if u == 0:
                wait(act, L.pv_done, step - 1)
            lo = 3 * WIN * u if L.local and u < 3 else 512 * u
            act.activation(pb[:, :, :].rearrange("p u c -> p (u c)")[:, lo:lo + cols], bank[:, 0:cols], ACT.Exp,
                           scale=SCALE).then_inc(L.exp_done, 1)

        if th.first:
            keep_xt(0)
        for j in range(4):
            if j == 0 and th.finish:
                keep_pv()
            for u in range(L.units):
                if th.pass2[j]:
                    exp(j, u)
                if j == 1 and u == 0 and th.finish:
                    keep_ot()
                if j == 3 and u in (0, 2) and th.prep:
                    keep_stack(1, u // 2)
                if j == 3 and u == 0 and th.turn_x:
                    keep_xt(i + 2)
                if u == L.units - 1 and th.max_step(j):
                    keep_mx(j)
            if j < 2 and th.prep:
                split_hi(j)
            if j in (1, 2) and th.prep:
                keep_stack(0, j - 1)

    iterations(act, body)


def attention_dve(dve, L, T, W, x_all_in=None):

    def body(i, p, th):
        n = 1 - p
        fin = i - 2

        def normalise():
            heads = T.mi[1][:, :].rearrange("p (h c) -> p h c", c=16)
            on = T.on[:, :, :].rearrange("p a (h d) -> p (a h) d", d=DH)
            dve.wait_ge(L.ot_done, L.kept * fin + 1)
            wait(dve, L.ont_done, fin)
            if not L.local:
                dve.reciprocal(T.rd[:, 0, :], heads[:, :, DH]).then_inc(L.rden, 1)
                dve.wait_ge(L.rden, fin + 1)
                dve.tensor_tensor(on, heads[:, :, 0:DH],
                                  T.rd[:, 0, :].rearrange("p (h o) -> p h o", o=1).to_broadcast([P, 32, DH]),
                                  ALU.mult).then_inc(L.on_done, 1)
                return
            glob = T.mi[0][:, :].rearrange("p (h c) -> p h c", c=16)
            ong = T.ong[:, :].rearrange("p (h d) -> p h d", d=DH)
            dve.reciprocal(T.rd[:, 0, :], heads[:, :, DH]).then_inc(L.rden, 1)
            dve.wait_ge(L.ot_done, L.kept * fin + 2)
            dve.reciprocal(T.rd[:, 1, :], glob[:, :, DH]).then_inc(L.rden, 1)
            dve.wait_ge(L.rden, 2 * fin + 1)
            dve.tensor_tensor(on, heads[:, :, 0:DH],
                              T.rd[:, 0, :].rearrange("p (h o) -> p h o", o=1).to_broadcast([P, 32, DH]),
                              ALU.mult).then_inc(L.on_half, 1)
            dve.wait_ge(L.rden, 2 * fin + 2)
            dve.tensor_tensor(ong, glob[:, :, 0:DH],
                              T.rd[:, 1, :].rearrange("p (h o) -> p h o", o=1).to_broadcast([P, 32, DH]),
                              ALU.mult).then_inc(L.on_half, 1)
            dve.wait_ge(L.on_half, 2 * fin + 2)
            dve.tensor_tensor(on, on, ong, ALU.add).then_inc(L.on_done, 1)

        def keep_vg():
            dve.wait_ge(L.vg_done, i + 1)
            wait(dve, L.pv_done, 4 * (i - 1))
            vg = T.mi[1][:, 0:D].rearrange("p (t r s d) -> p r s t d", t=4, r=2, s=2)
            out = T.vgb[p][:, :, :].rearrange("p (r s) (t z c) -> p r s t z c", r=2, t=4, z=2)
            mask = T.diag[:, :].rearrange("p (t d) -> p t d", t=4)
            for s in range(2):
                for r in range(2):
                    m = dve.tensor_tensor(out[:, r, s, :, s, 0:DH], vg[:, r, s, :, :], mask, ALU.mult)
            m.then_inc(L.vg_kept, 1)

        def keep_kg():
            dve.wait_ge(L.kg_done, i + 2)
            kg = T.mi[1][:, 0:4 * 32].rearrange("p (t g) -> p t g", t=4)
            for lo in (0, NGE + S):
                dve.tensor_copy(T.ks[n][:, :, lo:lo + NGE], kg[:, :, 0:NGE])
            dve.tensor_scalar(T.kg[n][:, :, 0:NG], kg[:, :, 0:NG], T.rows[:, 0:1], None,
                              ALU.add).then_inc(L.kg_kept, 1)

        def keep_pj(tau):
            dve.wait_ge(L.pj_done, 2 * (i + 1) + tau + 1)
            wait(dve, L.ts_done, 2 * i + tau + 1)
            mi = T.mi[tau]
            if not L.local:
                qk = mi[:, 0:2 * D].rearrange("p (h a f) -> p h a f", h=32, a=2)
                rs = T.rs[:, tau, :].rearrange("p (h a f) -> p h a f", h=32, a=2)
                cos = T.cos[:, tau, :].rearrange("p (o d) -> p o d", o=1)
                sin = T.sin[:, tau, :].rearrange("p (o a f) -> p o a f", o=1, a=2)
                dve.tensor_tensor(T.rq[:, tau, :].rearrange("p (h d) -> p h d", h=32),
                                  mi[:, 0:2 * D].rearrange("p (h d) -> p h d", h=32),
                                  cos.to_broadcast([P, 32, DH]), ALU.mult)
                dve.tensor_tensor(rs, qk[:, :, ::-1, :], sin.to_broadcast([P, 32, 2, DH // 2]), ALU.mult)
            else:
                dve.tensor_tensor(T.rq[:, tau, :], mi[:, 0:2 * D], W.bqkv[:, 0:2 * D], ALU.add).then_inc(L.sum_done, 1)
            wait(dve, L.vpad, i)
            if L.local:
                wait(dve, L.vg_done, i)
                dve.tensor_tensor(T.vtmp[:, n, tau, :], mi[:, 2 * D:3 * D], W.bqkv[:, 2 * D:3 * D],
                                  ALU.add).then_inc(L.pj_kept, 1)
            else:
                dve.tensor_copy(T.vtmp[:, n, tau, :], mi[:, 2 * D:3 * D]).then_inc(L.pj_kept, 1)

        def maxima(j, u):
            step = 4 * i + j
            bank = T.s1[u % L.ring1]
            if u == 0:
                wait(dve, L.msp_done, step - 1)
            wait_apart(dve, L.passed, L.p1_done, L.units * step + u + 1)
            nm = T.nm[:, j % 2, 0, :]

            def masked_maximum(item, at, mask):
                return dve.tensor_tensor_reduce(at, at, mask, -1.0, -BIG, ALU.add, ALU.min, nm[:, item:item + 1])

            if L.local:
                for c in range(2):
                    item = 2 * u + c
                    lo = c * WG + (0 if item // 4 else NGE)
                    masked_maximum(item, bank[:, lo:lo + WIN], T.band[:, item // 4, :])
                lo = 0 if u < 2 else WIN
                m = dve.tensor_reduce(T.nm[:, j % 2, 1, 2 * u:2 * u + 2],
                                      bank[:, 0:2 * WG].rearrange("p (h k) -> p h k", k=WG)[:, :, lo:lo + NG],
                                      AX.X, ALU.max, negate=True)
            elif u == 0:
                for t in range(4):
                    m = masked_maximum(t, bank[:, t * P:(t + 1) * P], T.causal[:, P:S])
            else:
                for c in range(2):
                    m = masked_maximum(2 + 2 * u + c, bank[:, c * S:(c + 1) * S], T.causal[:, :])
            m.then_inc(L.red_done, 1)

        def residual():
            dve.wait_ge(L.y_done, fin + 1)
            wait(dve, L.x_out, 2 * fin)
            if x_all_in is not None:
                dve.wait_ge(x_all_in, 48)
            resid = W.resid[:, bass.ds(2 * fin, 2), :]
            if L.local:
                dve.wait_ge(L.xb_done, fin + 1)
                resid = T.xb[:, :, :]
            dve.tensor_tensor(T.r[:, :, :], T.mi[0][:, 0:S].rearrange("p (a d) -> p a d", a=2), resid,
                              ALU.add).then_inc(L.r_done, 1)
            dve.wait_ge(L.r_done, fin + 1)
            wait(dve, L.aggr, 2 * fin)
            for tau in range(2):
                dve.bn_stats(T.st[:, tau, :], T.r[:, tau, :]).then_inc(L.stats, 1)
            wait(dve, L.rstd, fin)
            for tau in range(2):
                wait_apart(dve, L.passed, L.stats, 2 * fin + tau + 1)
                dve.bn_aggr(T.mv[:, tau, :], T.st[:, tau, :]).then_inc(L.aggr, 1)

        def layernorm():
            dve.wait_ge(L.rstd, fin + 1)
            for tau in range(2):
                dve.tensor_scalar(W.x_next[:, bass.ds(2 * fin + tau, 1), :], T.r[:, tau:tau + 1, :],
                                  T.mv[:, tau, 0:1], T.rs2[:, tau:tau + 1],
                                  ALU.subtract, ALU.mult).then_inc(L.x_out, 1)

        for j in range(4):
            for u in range(L.units):
                if th.scores:
                    maxima(j, u)
                if j in (0, 1) and u == 0 and th.prep:
                    keep_pj(j)
                if j == 0 and u == L.units - 2 and th.finish:
                    normalise()
                if j == 2 and u == (2 if L.local else 0) and th.finish:
                    residual()
                if j == 2 and u == 1 and L.local and th.scores:
                    keep_vg()
                if j == 3 and u == 2 and th.finish:
                    layernorm()
        if L.local and th.prep:
            keep_kg()

    iterations(dve, body)


def attention_pool(pool, L, T, W):

    def body(i, p, th):
        fin = i - 2

        def lay_out_v():
            wait_apart(pool, L.passed, L.pj_kept, 2 * i + 2)
            wait_apart(pool, L.passed, L.pv_done, 4 * (i - 1))
            v = T.vtmp[:, p, :, :].rearrange("p k (t r s d) -> p k s r t d", t=4, r=2, s=2)
            out = T.vb[p][:, :, :, :, :].rearrange("p k (r s) t (z c) -> p k s r t z c", r=2, z=2)
            for kt in range(2):
                for s in range(2):
                    m = pool.tensor_copy(out[:, kt, s, :, :, s, 0:DH], v[:, kt, s])
            m.then_inc(L.vpad, 1)

        def split_maxima(j):
            step = 4 * i + j - 1
            js = (j + 1) % 2
            wait_apart(pool, L.passed, L.red_done, L.units * (step + 1))
            wait_apart(pool, L.passed, L.mx_done, step - 1)
            nm = T.nm[:, js, :, :].rearrange("p g (a t) -> p g a t", a=2)
            msp = T.msp[:, js, :, 0:4 * L.parts].rearrange("p a (c t) -> p a c t", t=4)
            mspr = T.mspr[:, js, :, 0:4 * L.parts].rearrange("p a (c t) -> p a c t", t=4)
            if L.local:
                dm = T.dm[:, js, :].rearrange("p (a t) -> p a t", a=2)
                pool.tensor_tensor(dm, nm[:, 1], nm[:, 0], ALU.subtract).then_inc(L.msp_hi, 1)
            pool.tensor_copy(mspr[:, :, 0, :], nm[:, 0]).then_inc(L.msp_hi, 1)
            if L.local:
                wait_apart(pool, L.passed, L.msp_hi, 3 * step + 1)
                pool.tensor_copy(mspr[:, :, 2, :], dm).then_inc(L.msp_hi, 1)
                pool.wait_ge(L.msp_hi, 3 * step + 3)
                pool.tensor_tensor(mspr[:, :, 3, :], dm, msp[:, :, 2, :], ALU.subtract)
            else:
                pool.wait_ge(L.msp_hi, step + 1)
            pool.tensor_tensor(mspr[:, :, 1, :], nm[:, 0], msp[:, :, 0, :], ALU.subtract).then_inc(L.msp_done, 1)

        def add_rotated(tau):
            pool.wait_ge(L.pj_kept, 2 * (i + 1) + tau + 1)
            pool.tensor_tensor(T.rq[:, tau, :], T.rq[:, tau, :], T.rs[:, tau, :], ALU.add).then_inc(L.sum_done, 1)

        def split_lo(tau):
            pool.wait_ge(L.hi_done, 2 * (i + 1) + tau + 1)
            ts = T.ts[:, tau, :].rearrange("p (h c d) -> p h c d", h=32, d=DH)
            tsr = T.tsr[:, tau, :].rearrange("p (h c d) -> p h c d", h=32, d=DH)
            rq = T.rq[:, tau, :].rearrange("p (h d) -> p h d", h=32)
            pool.tensor_tensor(tsr[:, 0:16, 1, :], rq[:, 0:16], ts[:, 0:16, 0, :], ALU.subtract)
            pool.tensor_tensor(tsr[:, 16:32, 2, :], rq[:, 16:32], ts[:, 16:32, 0, :],
                               ALU.subtract).then_inc(L.ts_done, 1)

        def mask(j, u):
            step = 4 * i + j - 3
            pb = T.p[(j + 1) % 2][:, u, :]
            wait_apart(pool, L.passed, L.exp_done, 3 * step + u + 1)
            heads = 4 if u == 0 else 2
            at = pb.rearrange("p (h q) -> p h q", h=heads)[:, :, 0:P]
            pool.affine_select(out=at, in_=at, compare_op=ALU.is_ge, fill=0.0, base=0,
                               pattern=[[0, heads], [1, P]], channel_multiplier=-1).then_inc(L.masked, 1)

        def mask_window():
            step = 4 * i + j - 3
            pb = T.p[(j + 1) % 2][:, :, :].rearrange("p u c -> p (u c)")
            for late in range(2):
                for kt in range(2):
                    if late:
                        wait_apart(pool, L.passed, L.masked, 4 * step + kt + 1)
                    else:
                        wait_apart(pool, L.passed, L.exp_done, 4 * step + kt + 2)
                    first = (-HALF, 0)[kt]
                    lo, hi = (first + 2 * HALF + 1, WIN) if late else (0, P - 1 + first)
                    at = pb[:, 4 * kt * WIN:4 * (kt + 1) * WIN].rearrange("p (t q) -> p t q", t=4)[:, :, lo:hi]
                    sign = -1 if late else 1
                    base = -1 if late else -first
                    pool.affine_select(out=at, in_=at, compare_op=ALU.is_ge, fill=0.0, base=base,
                                       pattern=[[0, 4], [sign, hi - lo]],
                                       channel_multiplier=-sign).then_inc(L.masked, 1)

        def add_bias():
            wait_apart(pool, L.passed, L.r_done, fin)
            pool.tensor_tensor(T.xb[:, :, :], W.resid[:, bass.ds(2 * fin, 2), :],
                               W.bo[:].rearrange("p (o d) -> p o d", o=1).to_broadcast([P, 2, D]),
                               ALU.add).then_inc(L.xb_done, 1)

        def inverse_deviation():
            wait_apart(pool, L.passed, L.aggr, 2 * fin + 2)
            wait_apart(pool, L.passed, L.x_out, 2 * fin)
            pool.tensor_scalar(T.ve[:, :], T.mv[:, :, 1], EPS, None, ALU.add).then_inc(L.var_eps, 1)
            pool.wait_ge(L.var_eps, fin + 1)
            pool.tensor_tensor(T.rs2[:, :], T.ve[:, :], T.mhalf[:, 0:2], ALU.pow).then_inc(L.rstd, 1)

        for j in range(4):
            if th.max_step(j):
                split_maxima(j)
            if j == 1 and th.prep:
                split_lo(0)
            if j == 2 and th.prep:
                split_lo(1)
            if j == 2 and L.local and th.finish:
                add_bias()
            if j < 2 and th.prep and not L.local:
                add_rotated(j)
            if not L.local and th.pass2[j]:
                for u in range(3):
                    mask(j, u)
            if L.local and th.pass2[j]:
                mask_window()
            if j == 2 and th.finish:
                inverse_deviation()
            if j == 3 and th.scores:
                lay_out_v()

    iterations(pool, body)


def attention_sp(sp, L, T, W):

    def body(i, p, th):
        def load(batch, par):
            sp.dma_start(T.xin[:, par, :, :], W.x_batch(batch)).then_inc(L.x_in[par], 16)

        if isinstance(i, int) and i == -1:
            load(0, 0)
            load(1, 1)
        elif th.turn_x:
            sp.wait_ge(L.xt_done, i + 1)
            load(i + 2, p)
        def spread_queries():
            wait_apart(sp, L.passed, L.q_kept, 2 * i + 4)
            wait_apart(sp, L.passed, L.p2_done, 4 * i * L.units)
            for j in range(4):
                sp.dma_start(T.qs[1 - p][j][32 * j:32 * j + 32, :, :].bitcast(F32),
                             T.qf[32 * j:32 * j + 32, :, :].bitcast(F32)).then_inc(L.q_in[j], 16)

        for j in range(4):
            if th.max_step(j):
                js = (j + 3) % 4
                q = T.qs[(1 - p) if j == 0 else p][js]
                sp.wait_ge(L.mx_kept, 4 * i + j)
                sp.dma_start(q[32 * js + 24:32 * js + 24 + L.parts, :, :].bitcast(F32),
                             T.mt[js][0:4 * L.parts, :].bitcast(F32)).then_inc(L.mrow[js], 16)
            if j == 2 and th.prep:
                spread_queries()

    iterations(sp, body)


E = 8
HID = 512
HC = HID // P
G4 = 4
GT = G4 * P
GROUPS = NT // G4


class Mixture:

    def __init__(self, name, two, sem, passed):
        self.two = two
        self.steps = 20 if two else 5

        def s(what):
            return sem(f"{name}_{what}")

        self.xf_in = [s("xf_in0"), s("xf_in1")]
        self.ft_done, self.ft_kept = s("ft_done"), s("ft_kept")
        self.gate_done = s("gate_done")
        self.route = s("route")
        self.gt_done, self.gt_kept = s("gt_done"), s("gt_kept")
        self.g_done = s("g_done")
        self.y_done = s("y_done")
        self.back_done = s("back_done")
        self.r_done = s("r_done")
        self.sum_done = self.r_done if two else s("sum_done")
        self.stats, self.aggr, self.var_eps = s("stats"), s("aggr"), s("var_eps")
        self.rstd, self.x_out = s("rstd"), s("x_out")
        self.passed = passed
        if two:
            self.xl_kept = s("xl_kept")
            self.exp_done = s("exp_done")
            self.b2_done, self.b2_kept = s("b2_done"), s("b2_kept")
            self.w_in = [s("w_in0"), s("w_in1")]
            self.w_hi, self.w_ready = s("w_hi"), s("w_ready")
            self.h_done, self.relu_done = s("h_done"), s("relu_done")
            self.hi_even, self.hi_odd = s("hi_even"), s("hi_odd")
            self.lo_done = s("lo_done")
            self.o_done = s("o_done")
            self.gb_kept = s("gb_kept")
            self.ym_done, self.acc_done = s("ym_done"), s("acc_done")
        else:
            self.xm_done = s("xm_done")
            self.yt_kept = s("yt_kept")


def groups(eng, prologue, body, epilogue):
    prologue()
    for g in range(2):
        body(g, g)
    with eng.Fori(2, GROUPS - 3, 2) as g:
        body(g, 0)
        body(g + 1, 1)
    for g in range(GROUPS - 2, GROUPS):
        body(g, g % 2)
    epilogue()


def has_next(g):
    return not isinstance(g, int) or g + 1 < GROUPS


def has_last(g):
    return not isinstance(g, int) or g > 0


def mixture_sp(sp, M, T, x_from, W=None):

    def load_weights(e):
        wait(sp, M.w_ready, 2 * (e - 1))
        sp.dma_start(W.stage[e % 2], W.w_dram[e, :, :]).then_inc(M.w_in[e % 2], 16)

    def prologue():
        load(0, 0)
        if M.two:
            load_weights(0)
            load_weights(1)

    def load(g, p):
        wait(sp, M.ft_done, g - 1)
        sp.dma_start(T.xf[p][:, :, :], x_from[:, bass.ds(G4 * g, G4), :]).then_inc(M.xf_in[p], 16)

    def body(g, p):
        if has_next(g):
            load(g + 1, 1 - p)
        if M.two and isinstance(g, int) and g == 0:
            for e in range(2, E):
                load_weights(e)

    groups(sp, prologue, body, lambda: None)


def turn_tokens(pe, M, T, g, p):
    pe.wait_ge(M.xf_in[p], 8 * (g - p) + 16)
    wait(pe, M.ft_kept, g)
    wait(pe, M.r_done, g - 2)
    for a in range(G4):
        m = pe.transpose(T.mi[0][:, a * P:(a + 1) * P], T.xf[p][:, a, :], T.ident[:])
    m.then_inc(M.ft_done, 1)


def gate(pe, M, T, g, p, w):
    pe.wait_ge(M.ft_kept, g + 1)
    wait(pe, M.b2_kept if M.two else M.gt_kept, g)
    for a in range(G4):
        m = pe.matmul(T.mi[1][:, a * E:(a + 1) * E], T.xt4[p][:, a * P:(a + 1) * P], w,
                      start=a == 0, stop=True, skip_group_check=True)
    m.then_inc(M.gate_done, 1)


def turn_gates(pe, M, T, g):
    rows = 2 * E if M.two else E
    pe.wait_ge(M.route, M.steps * (g + 1))
    for a in range(G4):
        m = pe.transpose(T.mi[1][0:rows, a * P:(a + 1) * P].bitcast(F32R), T.gs[:, a, 0:rows], T.identr[:])
    m.then_inc(M.gt_done, 1)


def spread_gates(pe, M, T, g, p, e):
    if e == 0:
        pe.wait_ge(M.gt_kept, g + 1)
    wait(pe, M.gb_kept if M.two else M.xm_done, E * g + e - 1)
    pe.matmul(T.gb[e % 2][:, :], T.sel[:, e * P:(e + 1) * P], T.gt[p][:, :],
              start=True, stop=True).then_inc(M.g_done, 1)


def keep_gates(act, M, T, g, p):
    rows = 2 * E if M.two else E
    act.wait_ge(M.gt_done, g + 1)
    wait(act, M.g_done, E * (g - 1))
    act.copy(T.gt[p][0:rows, :], T.mi[1][0:rows, :]).then_inc(M.gt_kept, 1)


def turn_back(pe, M, T, g, turned):
    if isinstance(g, int) and g == GROUPS - 1:
        pe.wait_ge(M.r_done, g)
    else:
        pe.wait_ge(M.ft_kept, min(g + 3, GROUPS) if isinstance(g, int) else g + 3)
    for a in range(G4):
        m = pe.transpose(T.mi[0][:, a * P:(a + 1) * P], turned[:, a * P:(a + 1) * P], T.ident[:])
    m.then_inc(M.back_done, 1)


def residual_group(dve, M, T, g, x_from):
    total = T.sum[:, :, :]
    x = x_from[:, bass.ds(G4 * g, G4), :]
    dve.wait_ge(M.back_done, g + 1)
    wait(dve, M.x_out, G4 * g)
    dve.tensor_tensor(total, T.mi[0][:, :].rearrange("p (a d) -> p a d", a=G4), x, ALU.add).then_inc(M.r_done, 1)
    if not M.two:
        dve.wait_ge(M.r_done, g + 1)
        dve.tensor_tensor(total, total, x, ALU.add).then_inc(M.sum_done, 1)


def statistics_group(dve, M, T, g):
    dve.wait_ge(M.sum_done, g + 1)
    wait(dve, M.aggr, G4 * g)
    for a in range(G4):
        dve.bn_stats(T.st4[:, a, :], T.sum[:, a, :]).then_inc(M.stats, 1)
    wait(dve, M.rstd, g)
    for a in range(G4):
        wait_apart(dve, M.passed, M.stats, G4 * g + a + 1)
        dve.bn_aggr(T.mv4[:, a, :], T.st4[:, a, :]).then_inc(M.aggr, 1)


def scale_group(dve, M, T, g, x_to):
    dve.wait_ge(M.rstd, g + 1)
    for a in range(G4):
        dve.tensor_scalar(x_to[:, bass.ds(G4 * g + a, 1), :], T.sum[:, a:a + 1, :],
                          T.mv4[:, a, 0:1], T.rs4[:, a:a + 1], ALU.subtract, ALU.mult).then_inc(M.x_out, 1)


def inverse_deviation_group(pool, M, T, g):
    wait_apart(pool, M.passed, M.aggr, G4 * (g + 1))
    wait_apart(pool, M.passed, M.x_out, G4 * g)
    pool.tensor_scalar(T.ve4[:, :], T.mv4[:, :, 1], EPS, None, ALU.add).then_inc(M.var_eps, 1)
    pool.wait_ge(M.var_eps, g + 1)
    pool.tensor_tensor(T.rs4[:, :], T.ve4[:, :], T.mhalf[:, :], ALU.pow).then_inc(M.rstd, 1)


def spread(column, width):
    n = column.shape[1]
    return column.rearrange("p (a o) -> p a o", o=1).to_broadcast([P, n, width])


def choose(dve, M, T, scores, best, chosen, at):
    dve.tensor_reduce(best, scores, AX.X, ALU.max).then_inc(M.route, 1)
    dve.wait_ge(M.route, at + 1)
    dve.tensor_tensor(T.eq[:, :, :], scores, spread(best, E), ALU.is_ge).then_inc(M.route, 1)
    dve.wait_ge(M.route, at + 2)
    dve.tensor_tensor(T.rank[:, :, :], T.eq[:, :, :], T.first[:, :].rearrange("p (a e) -> p a e", e=E),
                      ALU.mult).then_inc(M.route, 1)
    dve.wait_ge(M.route, at + 3)
    dve.tensor_reduce(T.top[:, :], T.rank[:, :, :], AX.X, ALU.max).then_inc(M.route, 1)
    dve.wait_ge(M.route, at + 4)
    dve.tensor_tensor(chosen, T.rank[:, :, :], spread(T.top[:, :], E), ALU.is_equal).then_inc(M.route, 1)


def one_expert_pe(pe, M, T, W):

    def prepare(g, p, part):
        if part == 0:
            turn_tokens(pe, M, T, g, p)
        elif part == 1:
            gate(pe, M, T, g, p, W.gate[:])
        else:
            turn_gates(pe, M, T, g)

    def prologue():
        for part in range(3):
            prepare(0, 0, part)
        for e in range(2):
            spread_gates(pe, M, T, 0, 0, e)

    def back(g, p):
        pe.wait_ge(M.yt_kept, g + 1)
        turn_back(pe, M, T, g, T.yt)

    def body(g, p):
        for e in range(E):
            if e + 2 < E:
                spread_gates(pe, M, T, g, p, e + 2)
            elif has_next(g):
                spread_gates(pe, M, T, g + 1, 1 - p, e + 2 - E)
            if e == 0:
                wait(pe, M.yt_kept, g - 1)
            pe.wait_ge(M.xm_done, E * g + e + 1)
            pe.matmul(T.yb[p][:, :], W.expert[:, e * D:(e + 1) * D], T.xm[e % 4], start=e == 0,
                      stop=e == E - 1).then_inc(M.y_done, 1)
            if e in (0, 1, 4) and has_next(g):
                prepare(g + 1, 1 - p, (0, 1, 4).index(e))
            if e == 2 and has_last(g):
                back(g - 1, 1 - p)

    groups(pe, prologue, body, lambda: back(GROUPS - 1, (GROUPS - 1) % 2))


def one_expert_act(act, M, T):

    def keep_tokens(g, p):
        act.wait_ge(M.ft_done, g + 1)
        wait(act, M.xm_done, E * (g - 1))
        act.copy(T.xt4[p][:, :], T.mi[0][:, :]).then_inc(M.ft_kept, 1)

    def keep_outputs(g, p):
        act.wait_ge(M.y_done, E * (g + 1))
        wait(act, M.back_done, g)
        act.copy(T.yt[:, :], T.yb[p][:, :]).then_inc(M.yt_kept, 1)

    def prologue():
        keep_tokens(0, 0)
        keep_gates(act, M, T, 0, 0)

    def body(g, p):
        if has_next(g):
            keep_tokens(g + 1, 1 - p)
            keep_gates(act, M, T, g + 1, 1 - p)
        keep_outputs(g, p)

    groups(act, prologue, body, lambda: None)


def one_expert_dve(dve, M, T, x_from, x_to):

    def route(g):
        dve.wait_ge(M.gate_done, g + 1)
        wait(dve, M.gt_done, g)
        choose(dve, M, T, T.mi[1][:, 0:G4 * E].rearrange("p (a e) -> p a e", e=E), T.best[:, :],
               T.gs[:, :, 0:E], M.steps * g)

    def body(g, p):
        for e in range(E):
            dve.wait_ge(M.g_done, E * g + e + 1)
            wait(dve, M.y_done, E * g + e - 3)
            dve.tensor_tensor(T.xm[e % 4], T.xt4[p][:, :], T.gb[e % 2][:, :], ALU.mult).then_inc(M.xm_done, 1)
            if e == 3 and has_next(g):
                route(g + 1)
            if e == 4 and has_last(g):
                residual_group(dve, M, T, g - 1, x_from)
            if e == 5 and has_last(g):
                statistics_group(dve, M, T, g - 1)
            if e == 7 and has_last(g):
                scale_group(dve, M, T, g - 1, x_to)

    def epilogue():
        residual_group(dve, M, T, GROUPS - 1, x_from)
        statistics_group(dve, M, T, GROUPS - 1)
        scale_group(dve, M, T, GROUPS - 1, x_to)

    groups(dve, lambda: route(0), body, epilogue)


def mixture_pool(pool, M, T):

    def add(g, p, e):
        wait(pool, M.acc_done, E * g + e)
        if e == 0:
            pool.wait_ge(M.b2_kept, g + 1)
        pool.wait_ge(M.ym_done, E * g + e + 1)
        pool.tensor_tensor(T.acc[p], T.acc[p], T.ym[e % 2], ALU.add).then_inc(M.acc_done, 1)

    def body(g, p):
        if has_last(g):
            if M.two:
                add(g - 1, 1 - p, E - 1)
            inverse_deviation_group(pool, M, T, g - 1)
        if M.two:
            for e in range(E - 1):
                add(g, p, e)

    def epilogue():
        if M.two:
            add(GROUPS - 1, (GROUPS - 1) % 2, E - 1)
        inverse_deviation_group(pool, M, T, GROUPS - 1)

    groups(pool, lambda: None, body, epilogue)


def two_experts_pe(pe, M, T, W):

    def three(out, w_hi, w_lo, x_hi, x_lo, start, stop):
        pe.matmul(out, w_hi, x_hi, start=start, stop=False)
        pe.matmul(out, w_hi, x_lo, start=False, stop=False)
        return pe.matmul(out, w_lo, x_hi, start=False, stop=stop)

    def prepare(g, p, part):
        if part == 0:
            turn_tokens(pe, M, T, g, p)
        elif part == 1:
            gate(pe, M, T, g, p, W.router[:])
        elif part == 2:
            turn_gates(pe, M, T, g)
        else:
            pe.wait_ge(M.gt_kept, g + 1)
            pe.matmul(T.mi[1][:, :], W.b2_hi[:, :], T.gt[p][0:2 * E, :], start=True, stop=False)
            pe.matmul(T.mi[1][:, :], W.b2_lo[0:E, :], T.gt[p][0:E, :], start=False,
                      stop=True).then_inc(M.b2_done, 1)

    def hidden(g, p, n):
        e, c = divmod(n, HC)
        if n == 0:
            pe.wait_ge(M.xl_kept, g + 1)
        if isinstance(g, int) and g == 0 and c == 0:
            pe.wait_ge(M.w_ready, 2 * (e + 1))
        if n % 2:
            wait(pe, M.relu_done, E * HC * g + n - 1)
        else:
            wait(pe, M.hi_even, E * HC // 2 * g + n // 2)
        three(T.hb[n % 2][:, :], W.hi[e][:, c * P:(c + 1) * P], W.lo[e][:, c * P:(c + 1) * P], T.xh[p], T.xl[p],
              True, True).then_inc(M.h_done, 1)

    def out(g, p, n):
        e, c = divmod(n, HC)
        if c == 0:
            wait(pe, M.ym_done, E * g + e - 1)
        pe.wait_ge(M.lo_done, E * HC * g + n + 1)
        m = three(T.yb[e % 2][:, :], W.hi[e][:, HID + c * P:HID + (c + 1) * P], W.lo[e][:, HID + c * P:HID + (c + 1) * P],
                  T.hh[n % 4], T.hl[n % 4], c == 0, c == HC - 1)
        m.then_inc(M.o_done, 1)

    def back(g, p):
        pe.wait_ge(M.acc_done, E * (g + 1))
        turn_back(pe, M, T, g, T.acc[p])

    def prologue():
        for part in range(4):
            prepare(0, 0, part)
        for n in range(2):
            hidden(0, 0, n)

    def body(g, p):
        for n in range(E * HC):
            if n % HC == 0:
                spread_gates(pe, M, T, g, p, n // HC)
            if n + 2 < E * HC:
                hidden(g, p, n + 2)
            elif has_next(g):
                hidden(g + 1, 1 - p, n + 2 - E * HC)
            out(g, p, n)
            if n == 2 and has_next(g):
                prepare(g + 1, 1 - p, 0)
            if n == 6 and has_last(g):
                back(g - 1, 1 - p)
            if n in (8, 22, 25) and has_next(g):
                prepare(g + 1, 1 - p, (0, 8, 22, 25).index(n))

    groups(pe, prologue, body, lambda: back(GROUPS - 1, (GROUPS - 1) % 2))


def two_experts_act(act, M, T, W):

    def prepare(g, p, part):
        if part == 0:
            act.wait_ge(M.ft_done, g + 1)
            wait(act, M.h_done, E * HC * (g - 1))
            act.copy(T.xh[p], T.mi[0][:, :])
            act.copy(T.xt4[p][:, :], T.mi[0][:, :]).then_inc(M.ft_kept, 1)
        elif part == 1:
            act.wait_ge(M.route, M.steps * g + 13)
            act.activation(T.e2[:, :], T.diff[:, :], ACT.Exp).then_inc(M.exp_done, 1)
        elif part == 2:
            keep_gates(act, M, T, g, p)
        else:
            act.wait_ge(M.b2_done, g + 1)
            wait(act, M.back_done, g - 1)
            act.copy(T.acc[p], T.mi[1][:, :]).then_inc(M.b2_kept, 1)

    def upper_weights(e):
        act.wait_ge(M.w_in[e % 2], 16 * (e // 2 + 1))
        for part in range(2):
            cols = slice(part * HID, (part + 1) * HID)
            act.copy(W.hi[e][:, cols], W.stage[e % 2][:, cols]).then_inc(M.w_hi, 1)

    def prologue():
        upper_weights(0)
        for part in range(4):
            prepare(0, 0, part)

    def body(g, p):
        for n in range(E * HC):
            at = E * HC * g + n
            act.wait_ge(M.h_done, at + 1)
            wait(act, M.lo_done, at - 1)
            act.activation(T.relu[n % 2], T.hb[n % 2][:, :], ACT.Relu, bias=W.b1[:, n:n + 1]).then_inc(M.relu_done, 1)
            if n % 2 == 0:
                wait(act, M.o_done, at - 3)
                act.activation(T.hh[n % 4], T.hb[n % 2][:, :], ACT.Relu,
                               bias=W.b1[:, n:n + 1]).then_inc(M.hi_even, 1)
            if n in (5, 18, 25, 28) and has_next(g):
                prepare(g + 1, 1 - p, (5, 18, 25, 28).index(n))
            if n % HC == 0 and isinstance(g, int) and g == 0 and n // HC + 1 < E:
                upper_weights(n // HC + 1)

    groups(act, prologue, body, lambda: None)


def two_experts_dve(dve, M, T, W, x_from, x_to):

    def route(g, part):
        at = M.steps * g
        if part == 0:
            dve.wait_ge(M.gate_done, g + 1)
            dve.tensor_tensor(T.logits[:, :, :], T.mi[1][:, 0:G4 * E].rearrange("p (a e) -> p a e", e=E),
                              W.rb[:].rearrange("p (o e) -> p o e", o=1).to_broadcast([P, G4, E]),
                              ALU.add).then_inc(M.route, 1)
            dve.wait_ge(M.route, at + 1)
            choose(dve, M, T, T.logits[:, :, :], T.best[:, :], T.pick1[:, :, :], at + 1)
            return
        if part == 1:
            dve.wait_ge(M.route, at + 6)
            dve.scalar_tensor_tensor(T.logits[:, :, :], T.pick1[:, :, :], -1e38, T.logits[:, :, :],
                                     ALU.mult, ALU.add).then_inc(M.route, 1)
            dve.wait_ge(M.route, at + 7)
            choose(dve, M, T, T.logits[:, :, :], T.best2[:, :], T.pick2[:, :, :], at + 7)
            dve.wait_ge(M.route, at + 12)
            dve.tensor_tensor(T.diff[:, :], T.best2[:, :], T.best[:, :], ALU.subtract).then_inc(M.route, 1)
            return
        dve.wait_ge(M.exp_done, g + 1)
        dve.tensor_scalar(T.den[:, :], T.e2[:, :], 1.0, None, ALU.add).then_inc(M.route, 1)
        dve.wait_ge(M.route, at + 14)
        dve.reciprocal(T.g1[:, :], T.den[:, :]).then_inc(M.route, 1)
        dve.wait_ge(M.route, at + 15)
        dve.tensor_tensor(T.g2[:, :], T.e2[:, :], T.g1[:, :], ALU.mult).then_inc(M.route, 1)
        dve.wait_ge(M.route, at + 16)
        dve.tensor_tensor(T.pick1[:, :, :], T.pick1[:, :, :], spread(T.g1[:, :], E), ALU.mult)
        dve.tensor_tensor(T.pick2[:, :, :], T.pick2[:, :, :], spread(T.g2[:, :], E), ALU.mult).then_inc(M.route, 1)
        dve.wait_ge(M.route, at + 17)
        wait(dve, M.gt_done, g)
        dve.tensor_tensor(T.gates[:, :, :], T.pick1[:, :, :], T.pick2[:, :, :], ALU.add).then_inc(M.route, 1)
        dve.wait_ge(M.route, at + 18)
        dve.tensor_copy(T.gs[:, :, 0:E], T.gates[:, :, :]).then_inc(M.route, 1)
        dve.wait_ge(M.route, at + 19)
        dve.tensor_tensor(T.gs[:, :, E:2 * E], T.gates[:, :, :], T.gs[:, :, 0:E].bitcast(F32),
                          ALU.subtract).then_inc(M.route, 1)

    def lower_tokens(g, p):
        dve.wait_ge(M.ft_kept, g + 1)
        dve.tensor_tensor(T.xl[p], T.xt4[p][:, :], T.xh[p].bitcast(F32), ALU.subtract).then_inc(M.xl_kept, 1)

    def gated(g, e):
        dve.wait_ge(M.gb_kept, E * g + e + 1)
        wait(dve, M.acc_done, E * g + e - 1)
        dve.wait_ge(M.o_done, E * HC * g + HC * (e + 1))
        dve.tensor_tensor(T.ym[e % 2], T.yb[e % 2][:, :], T.gb_sb, ALU.mult).then_inc(M.ym_done, 1)

    def lower_weights(e):
        for part in range(2):
            cols = slice(part * HID, (part + 1) * HID)
            dve.wait_ge(M.w_hi, 2 * e + part + 1)
            dve.tensor_tensor(W.lo[e][:, cols], W.stage[e % 2][:, cols], W.hi[e][:, cols].bitcast(F32),
                              ALU.subtract).then_inc(M.w_ready, 1)

    def prologue():
        lower_weights(0)
        lower_tokens(0, 0)
        for part in range(3):
            route(0, part)

    def body(g, p):
        for n in range(E * HC):
            at = E * HC * g + n
            if n % 2:
                dve.wait_ge(M.relu_done, at + 1)
                wait(dve, M.o_done, at - 3)
                dve.tensor_copy(T.hh[n % 4], T.relu[n % 2]).then_inc(M.hi_odd, 1)
                dve.wait_ge(M.hi_odd, E * HC // 2 * g + n // 2 + 1)
            else:
                dve.wait_ge(M.hi_even, E * HC // 2 * g + n // 2 + 1)
            dve.tensor_tensor(T.hl[n % 4], T.relu[n % 2], T.hh[n % 4].bitcast(F32), ALU.subtract).then_inc(M.lo_done, 1)
            if n == 1 and has_last(g):
                gated(g - 1, E - 1)
            if n % HC == 1 and n > 1:
                gated(g, n // HC - 1)
            if n % HC == 2:
                e = n // HC
                dve.wait_ge(M.g_done, E * g + e + 1)
                wait(dve, M.ym_done, E * g + e)
                dve.tensor_copy(T.gb_sb, T.gb[e % 2][:, :]).then_inc(M.gb_kept, 1)
            if n == 7 and has_next(g):
                lower_tokens(g + 1, 1 - p)
            if n == 9 and has_last(g):
                residual_group(dve, M, T, g - 1, x_from)
            if n == 10 and has_last(g):
                statistics_group(dve, M, T, g - 1)
            if n == 12 and has_last(g):
                scale_group(dve, M, T, g - 1, x_to)
            if n in (14, 16, 20) and has_next(g):
                route(g + 1, (14, 16, 20).index(n))
            if n % HC == 0 and isinstance(g, int) and g == 0 and n // HC + 1 < E:
                lower_weights(n // HC + 1)

    def epilogue():
        gated(GROUPS - 1, E - 1)
        residual_group(dve, M, T, GROUPS - 1, x_from)
        statistics_group(dve, M, T, GROUPS - 1)
        scale_group(dve, M, T, GROUPS - 1, x_to)

    groups(dve, prologue, body, epilogue)


def tiled(a, width):
    return np.ascontiguousarray(a.reshape(2, P, width).transpose(1, 0, 2)).astype(np.float32)


def constants():
    causal = np.where(np.arange(P)[None, :] > np.arange(P)[:, None], BIG, 0.0)
    r, c, row = np.arange(P)[:, None], np.arange(WIN)[None, :], np.arange(P)
    band = [np.where(np.abs(r + off - c) <= HALF, 0.0, BIG) for off in (0, P - (S - WIN))]
    inv = (1.0 / np.float32(10000.0) ** (np.arange(0, DH, 2, dtype=np.float32) / np.float32(DH))).astype(np.float32)
    ang = np.arange(S, dtype=np.float32)[:, None] * inv[None, :]
    ninth = np.zeros((4, 32, 4, 4, 2, 16), np.float32)
    for t in range(4):
        for j in range(4):
            ninth[t, 0:NG, j, t, j % 2, DH] = 1.0 / W_GLOBAL
    return {
        "ident": np.eye(P),
        "causal": np.concatenate([np.zeros((P, P)), causal], axis=1),
        "band": np.stack(band, axis=1),
        "rows": ((row % 32 == 26) | (row % 32 == 27))[:, None],
        "cos": tiled(np.concatenate([np.cos(ang)] * 2, axis=1), DH),
        "sin": tiled(np.concatenate([-np.sin(ang), np.sin(ang)], axis=1), DH),
        "ninth": ninth.reshape(P, 4 * P),
        "diag": np.repeat(np.eye(4), 32, axis=0).repeat(DH, axis=1),
        "kidx": np.arange(2)[None, :] * P + np.arange(P)[:, None],
        "sel": np.repeat(np.tile(np.eye(E), (2, 1)), P, axis=1),
        "first": np.tile(np.arange(8, 0, -1), (P, 4)),
    }


class Tensors:
    pass


def build(nc, a):
    with ExitStack() as ctx:
        def sb(name, shape, dt=F32):
            return ctx.enter_context(nc.sbuf_tensor(name, shape, dt))

        def sem(name):
            return ctx.enter_context(nc.semaphore(name))

        bank = [ctx.enter_context(nc.psum_tensor(f"bank{i}", [P, 512], F32)) for i in range(8)]
        passed = sem("passed")
        T = Tensors()
        T.ident, T.identr = sb("ident", [P, P]), sb("identr", [P, P], F32R)
        T.causal, T.band, T.rows = sb("causal", [P, S]), sb("band", [P, 2, WIN]), sb("rows", [P, 1])
        T.cos, T.sin = sb("cos", [P, 2, DH]), sb("sin", [P, 2, DH])
        T.xin, T.xt = sb("xin", [P, 2, 2, D]), sb("xt", [P, S])
        T.rq, T.rs = sb("rq", [P, 2, 2 * D]), sb("rs", [P, 2, 2 * D])
        T.tsr = sb("ts", [P, 2, 8 * P], F32R)
        T.ts = T.tsr[:, :, :].bitcast(F32)
        T.vtmp, T.qf = sb("vtmp", [P, 2, 2, D]), sb("qf", [P, 4, S], F32R)
        T.vb = [sb(f"vb{i}", [P, 2, 4, 4, 32]) for i in range(2)]
        T.qs = [[sb(f"qs{i}_{j}", [P, 4, S], F32R) for j in range(4)] for i in range(2)]
        T.ks = [sb(f"ks{i}", [P, 4, KW], F32R) for i in range(2)]
        T.p = [sb(f"p{i}", [P, 4, 512]) for i in range(2)]
        T.nm, T.dm = sb("nm", [P, 2, 2, 8]), sb("dm", [P, 2, 8])
        T.mspr = sb("msp", [P, 2, 2, 16], F32R)
        T.msp = T.mspr[:, :, :, :].bitcast(F32)
        T.mt = [sb(f"mt{j}", [16, S], F32R) for j in range(4)]
        T.ovs, T.ogs = sb("ovs", [P, 2, S]), sb("ogs", [P, 2, S])
        T.rd = sb("rd", [P, 2, 32])
        T.on, T.ong, T.ot = sb("on", [P, 2, D]), sb("ong", [P, 2 * D]), sb("ot", [P, S])
        T.r, T.st, T.mv, T.rs2 = sb("r", [P, 2, D]), sb("st", [P, 2, 6]), sb("mv", [P, 2, 2]), sb("rs2", [P, 2])
        T.ve, T.mhalf = sb("ve", [P, 2]), sb("mhalf", [P, 4])
        T.kg = [sb(f"kg{i}", [P, 4, 32]) for i in range(2)]
        T.pick, T.pick4 = sb("pick", [P, 2, NGE], F32R), sb("pick4", [P, 2, 4, 32])
        T.vgb = [sb(f"vgb{i}", [P, 4, P]) for i in range(2)]
        T.diag = sb("diag", [P, 4 * DH])
        kidx, gi, gif = sb("kidx", [P, 2]), sb("gi", [P, NG], mybir.dt.int32), sb("gif", [P, NG])
        x_a, x_b = sb("x_a", [P, NT, D]), sb("x_b", [P, NT, D])

        T.xf = [sb("xf", [P, G4, D]).ap(), T.xin.ap().rearrange("p a b d -> p (a b) d")]
        T.xt4 = [sb(f"xt4_{i}", [P, GT]) for i in range(2)]
        T.sum, T.st4, T.mv4 = sb("sum", [P, G4, D]), sb("st4", [P, G4, 6]), sb("mv4", [P, G4, 2])
        T.ve4, T.rs4, T.first = sb("ve4", [P, G4]), sb("rs4", [P, G4]), sb("first", [P, G4 * E])
        T.eq, T.rank, T.gates, T.logits, T.pick1, T.pick2 = (
            sb(n, [P, G4, E]) for n in ("eq", "rank", "gates", "logits", "pick1", "pick2"))
        T.best, T.best2, T.top, T.diff, T.e2, T.den, T.g1, T.g2 = (
            sb(n, [P, G4]) for n in ("best", "best2", "top", "diff", "e2", "den", "g1", "g2"))
        T.gs, T.gt = sb("gs", [P, G4, 2 * E], F32R), [sb(f"gt{i}", [P, GT], F32R) for i in range(2)]
        T.sel = sb("sel", [P, E * P], F32R)
        T.yb, T.gb, T.hb = bank[4:6], bank[6:8], bank[2:4]

        def flat(t, width):
            whole = t.ap().rearrange("p u c -> p (u c)")
            return [whole[:, k * width:(k + 1) * width] for k in range(whole.shape[1] // width)]

        T.xm, T.yt = flat(T.p[0], GT), flat(T.p[1], GT)[0]
        T.hh, T.hl = flat(T.tsr, GT), flat(T.ks[0], GT)[0:2] + flat(T.ks[1], GT)[0:2]
        T.xh, T.xl = flat(T.qf, GT), [sb(f"xl{i}", [P, GT], F32R).ap() for i in range(2)]
        T.relu, T.gb_sb = flat(T.p[0], GT)[0:2], flat(T.p[0], GT)[2]
        T.acc, T.ym = flat(T.p[1], GT)[0:2], flat(T.p[1], GT)[2:4]
        F0, F1 = Mixture("f0", False, sem, passed), Mixture("f1", True, sem, passed)
        V0, V1 = Tensors(), Tensors()
        V0.gate, V0.expert = sb("gate", [P, E]), sb("expert", [P, E * D])
        V1.router, V1.rb, V1.b1, V1.b2 = sb("router", [P, E]), sb("rb", [P, E]), sb("b1", [P, E * HC]), sb("b2", [2 * E, D])
        V1.b2_hi, V1.b2_lo = sb("b2_hi", [2 * E, D], F32R), sb("b2_lo", [2 * E, D], F32R)
        V1.stage = [t.ap().rearrange("p k j t c -> p (k j t c)") for t in T.vb]
        V1.lo = [sb(f"w{e}", [P, 2 * HID], F32R).ap() for e in range(E)]
        V1.w_dram = a["w"]
        V1.hi = [T.qs[e // 4][e % 4].ap().rearrange("p t s -> p (t s)") for e in range(E)]
        T.mi, T.s1, T.ov = [bank[0], bank[1]], [bank[2], bank[3], bank[7]], bank[4]
        L0, L1 = Attention("l0", False, sem, passed), Attention("l1", True, sem, passed)
        T.s2, T.og = [bank[5], bank[6]], bank[7]
        x_dram = a["x"]
        W0, W1 = Tensors(), Tensors()
        W0.qkv, W0.out = sb("w0_qkv", [P, 3 * D]), sb("w0_out", [P, D])
        W0.x_batch = lambda b: x_dram[bass.ds(b, 1), :, :].rearrange("o (a p) d -> p (o a) d", p=P)
        W0.resid, W0.x_next = x_a, x_b
        W1.qkv, W1.out = sb("w1_qkv", [P, 3 * D]), sb("w1_out", [P, D])
        W1.bqkv, W1.bo, T.xb = sb("b1_qkv", [P, 3 * D]), sb("bo", [P, D]), sb("xb", [P, 2, D])

        const_in, x_a_in, stored = sem("const_in"), sem("x_a_in"), sem("stored")
        ready, zeroed, preset = sem("ready"), sem("zeroed"), sem("preset")
        once = sem("once")
        loads = [(T.ident, "ident"), (T.causal, "causal"), (T.band, "band"), (T.rows, "rows"), (W0.qkv, "w0_qkv"), (T.cos, "cos"), (T.sin, "sin"), (W0.out, "w0_out"),
                 (T.diag, "diag"), (T.first, "first"), (V0.gate, "gate"), (V0.expert, "expert"), (V1.router, "router"),
                 (V1.b1, "b1"), (V1.b2, "b2"), (kidx, "kidx"), (W1.qkv, "w1_qkv"), (W1.out, "w1_out")]
        sel = T.p[0].ap().rearrange("p u c -> p (u c)")[0:2 * E, 0:E * P]
        rows = [(gi, "gi"), (W1.bqkv, "b1_qkv"), (W1.bo, "bo"), (V1.rb, "rb")]
        n_const = 16 * (len(loads) + 1 + len(rows))
        W1.x_batch = lambda b: x_a[:, bass.ds(2 * b, 2), :]
        W1.resid, W1.x_next = x_a, x_b
        left = [(L1.pv_done, 4 * B), (L1.p2_done, 4 * 4 * B), (L1.ot_done, 2 * B), (L1.y_done, B)]
        block = ctx.enter_context(nc.Block())

        @block.sync
        def _(sp):
            for t, name in loads:
                sp.dma_start(t.ap(), a[name]).then_inc(const_in, 16)
            sp.dma_start(sel, a["sel"]).then_inc(const_in, 16)
            for t, name in rows:
                sp.dma_start(t.ap(), a[name].to_broadcast([P, a[name].shape[1]])).then_inc(const_in, 16)
            sp.dma_start(x_a[:, :, :], x_dram.rearrange("b (a p) d -> p (b a) d", p=P)).then_inc(x_a_in, 16)
            for g in T.vgb:
                sp.dma_start(g.ap(), a["ninth"].rearrange("p (j c) -> p j c", j=4)).then_inc(x_a_in, 16)
            attention_sp(sp, L0, T, W0)
            sp.wait_ge(L0.x_out, NT)
            mixture_sp(sp, F0, T, x_b)
            sp.wait_ge(F0.x_out, NT)
            attention_sp(sp, L1, T, W1)
            sp.wait_ge(L1.x_out, NT)
            for signal, value in left:
                sp.wait_ge(signal, value)
            mixture_sp(sp, F1, T, x_b, V1)
            out = a["out"].rearrange("b (a p) d -> p (b a) d", p=P)
            for g in range(GROUPS):
                sp.wait_ge(F1.x_out, G4 * (g + 1))
                sp.dma_start(out[:, G4 * g:G4 * (g + 1), :], x_a[:, G4 * g:G4 * (g + 1), :]).then_inc(stored, 16)
            sp.wait_ge(stored, 16 * GROUPS)

        @block.tensor
        def _(pe):
            pe.wait_ge(const_in, n_const)
            pe.wait_ge(ready, 3)
            pe.wait_ge(preset, 4)
            attention_pe(pe, L0, T, W0)
            pe.wait_ge(L0.exp_done, 3 * 4 * B)
            pe.wait_ge(L0.r_done, B)
            pe.wait_ge(L0.red_done, 3 * 4 * B)
            pe.wait_ge(once, 4)
            one_expert_pe(pe, F0, T, V0)
            pe.wait_ge(preset, 6)
            pe.wait_ge(F0.r_done, GROUPS)
            pe.wait_ge(F0.gt_kept, GROUPS)
            attention_pe(pe, L1, T, W1)
            pe.wait_ge(L1.exp_done, 4 * 4 * B)
            pe.wait_ge(L1.r_done, B)
            pe.wait_ge(L1.red_done, 4 * 4 * B)
            two_experts_pe(pe, F1, T, V1)

        @block.scalar
        def _(act):
            act.wait_ge(preset, 4)
            act.wait_ge(const_in, n_const)
            act.wait_ge(once, 3)
            attention_act(act, L0, T, W0)
            act.wait_ge(L0.pv_done, 4 * B)
            one_expert_act(act, F0, T)
            act.wait_ge(F0.back_done, GROUPS)
            attention_act(act, L1, T, W1)
            for signal, value in left:
                act.wait_ge(signal, value)
            two_experts_act(act, F1, T, V1)

        @block.vector
        def _(dve):
            dve.wait_ge(const_in, n_const)
            dve.tensor_copy(T.identr[:], T.ident[:]).then_inc(ready, 1)
            dve.tensor_copy(gif[:], gi[:]).then_inc(once, 1)
            dve.tensor_copy(V1.b2_hi[:], V1.b2[:]).then_inc(once, 1)
            dve.wait_ge(zeroed, 7)
            dve.tensor_copy(T.sel[0:2 * E, :], sel).then_inc(once, 1)
            dve.wait_ge(once, 3)
            dve.tensor_tensor(V1.b2_lo[:], V1.b2[:], V1.b2_hi[:].bitcast(F32), ALU.subtract).then_inc(once, 1)
            dve.wait_ge(zeroed, 7)
            for kt in range(2):
                dve.tensor_scalar(T.pick[:, kt, 0:NG], gif[:], kidx[:, kt:kt + 1], None,
                                  ALU.is_equal).then_inc(ready, 1)
            for kt in range(2):
                dve.tensor_scalar(T.pick4[:, kt, :, 0:NG], gif[:].rearrange("p (o g) -> p o g", o=1).to_broadcast([P, 4, NG]),
                                  kidx[:, kt:kt + 1], None, ALU.is_equal).then_inc(ready, 1)
            attention_dve(dve, L0, T, W0, x_a_in)
            dve.wait_ge(L0.pv_done, 4 * B)
            one_expert_dve(dve, F0, T, x_b, x_a)
            attention_dve(dve, L1, T, W1)
            for signal, value in left:
                dve.wait_ge(signal, value)
            two_experts_dve(dve, F1, T, V1, x_b, x_a)

        @block.gpsimd
        def _(pool):
            for t in (T.sel, *T.gt):
                pool.memset(t[:, :].bitcast(F32), 0.0)
            pool.memset(T.mhalf[:], -0.5).then_inc(zeroed, 1)
            pool.memset(T.pick[:, :, :].bitcast(F32), 0.0).then_inc(zeroed, 1)
            pool.memset(T.pick4[:, :, :, :], 0.0).then_inc(zeroed, 1)
            pool.memset(T.ts[:, :, :], 0.0).then_inc(zeroed, 1)
            for par in range(2):
                for j in range(4):
                    pool.memset(T.qs[par][j][:, :, :].bitcast(F32), 0.0)
            for par in range(2):
                pool.memset(T.vb[par][:, :, :, :, :], 0.0).then_inc(zeroed, 1)
            for par in range(2):
                m = pool.memset(T.kg[par][:, :, :], 0.0)
            m.then_inc(zeroed, 1)
            pool.wait_ge(zeroed, 7)
            keys = T.ts[:, :, :].rearrange("p a (h c) -> p a h c", c=32)[:, :, 16:32, 24:26]
            pool.memset(keys, 1.0).then_inc(preset, 1)
            pool.memset(T.mspr[:, :, :, :].bitcast(F32), 0.0).then_inc(preset, 1)

            def ninth_column(value, signal):
                for par in range(2):
                    for s in range(2):
                        m = pool.memset(T.vb[par][:, :, s::2, :, 16 * s + DH], value)
                    m.then_inc(signal, 1)

            ninth_column(1.0, preset)
            attention_pool(pool, L0, T, W0)
            mixture_pool(pool, F0, T)
            pool.wait_ge(L0.pv_done, 4 * B)
            ninth_column(1.0 / W_LOCAL, preset)
            pool.wait_ge(const_in, n_const)
            pool.wait_ge(F0.x_out, NT)
            attention_pool(pool, L1, T, W1)
            for signal, value in left:
                pool.wait_ge(signal, value)
            mixture_pool(pool, F1, T)


def out_rows(w):
    return np.ascontiguousarray(w.reshape(4, 2, 2, DH, D).transpose(1, 0, 2, 3, 4).reshape(D, D))


def kernel(L0_attn_x, L0_attn_w_qkv, L0_attn_w_out, L0_ffn_gate_w, L0_ffn_expert_w, L1_attn_Wq, L1_attn_bq,
           L1_attn_Wk, L1_attn_bk, L1_attn_Wv, L1_attn_bv, L1_attn_Wo, L1_attn_bo, L1_attn_global_indices,
           L1_ffn_router_w, L1_ffn_router_b, L1_ffn_w1, L1_ffn_b1, L1_ffn_w2, L1_ffn_b2):
    import concourse.bacc as bacc
    from concourse.bass_utils import run_bass_kernel_spmd

    def turned(w):
        return np.asarray(w).T

    arrays = {k: v.astype(np.float32) for k, v in constants().items()}
    arrays.update(
        x=L0_attn_x, w0_qkv=L0_attn_w_qkv, w0_out=out_rows(np.asarray(L0_attn_w_out)),
        gate=turned(L0_ffn_gate_w),
        expert=np.asarray(L0_ffn_expert_w).transpose(2, 0, 1).reshape(D, E * D),
        w1_qkv=np.concatenate([turned(L1_attn_Wq), turned(L1_attn_Wk), turned(L1_attn_Wv)], axis=1),
        b1_qkv=np.concatenate([L1_attn_bq, L1_attn_bk, L1_attn_bv])[None, :],
        w1_out=out_rows(turned(L1_attn_Wo)), bo=np.asarray(L1_attn_bo)[None, :],
        gi=np.asarray(L1_attn_global_indices)[None, :],
        router=L1_ffn_router_w, rb=np.asarray(L1_ffn_router_b)[None, :],
        w=np.concatenate([np.asarray(L1_ffn_w1), np.asarray(L1_ffn_w2).reshape(E, HC, P, D).transpose(0, 2, 1, 3)
                          .reshape(E, P, HID)], axis=2),
        b1=np.asarray(L1_ffn_b1).reshape(E * HC, P).T,
        b2=np.concatenate([L1_ffn_b2, L1_ffn_b2]))
    arrays = {k: np.ascontiguousarray(v) for k, v in arrays.items()}

    nc = bacc.Bacc("TRN2", target_bir_lowering=False, num_devices=1)
    a = {k: nc.dram_tensor(f"in_{k}", v.shape, mybir.dt.from_np(v.dtype), kind="ExternalInput").ap()
         for k, v in arrays.items()}
    a["out"] = nc.dram_tensor("result", (B, S, D), F32, kind="ExternalOutput").ap()
    build(nc, a)
    r = run_bass_kernel_spmd(nc, [{f"in_{k}": v for k, v in arrays.items()}], core_ids=[0])
    return r.results[0]["result"]
```
